# Optimizing a Trainium2 kernel written in Bass

```python
import numpy as np
import jax
import jax.numpy as jnp

def _softmax(x, axis=-1):
    return jax.nn.softmax(x, axis=axis)

def _gelu(x):
    return jax.nn.gelu(x, approximate=True)

def _silu(x):
    return jax.nn.silu(x)

def _sigmoid(x):
    return jax.nn.sigmoid(x)

def _layernorm(x, axis=-1, eps=1e-05):
    m = jnp.mean(x, axis=axis, keepdims=True)
    v = jnp.var(x, axis=axis, keepdims=True)
    return (x - m) / jnp.sqrt(v + eps)

def _scatter_add(tgt, idx, src, axis=0):
    return tgt.at[idx].add(src)

def _segment_sum(src, seg, n):
    return jax.ops.segment_sum(src, seg, n)
kernel_name = 'mk_cond_resid_d4_seqx_r8_a96619'

def setup_inputs(seed: int=0):
    np.random.seed(seed)
    _w = jnp.asarray

    def _rec_inputs():
        import jax
        import jax.numpy as jnp
        _rk = jax.random.key(seed)
        x = -0.000125 + 0.9999 * jax.random.normal(jax.random.fold_in(_rk, 1), (8, 128, 512), jnp.float32)
        _lenS = 128 - jax.random.randint(jax.random.fold_in(_rk, 7), (8,), 0, max(1, 128 // 4) + 1, jnp.int32)
        _lenS2 = 128 - jax.random.randint(jax.random.fold_in(_rk, 8), (8,), 0, max(1, 128 // 4) + 1, jnp.int32)
        itok_B_6_15 = jax.random.randint(jax.random.fold_in(_rk, 11), (8,), 6, 16, jnp.int32)
        itok_B_3_7 = jax.random.randint(jax.random.fold_in(_rk, 12), (8,), 3, 8, jnp.int32)
        itok_B_1_14 = jax.random.randint(jax.random.fold_in(_rk, 13), (8,), 1, 15, jnp.int32)
        condB_coeff = 0.00219231 + 0.0100837 * jax.random.normal(jax.random.fold_in(_rk, 14), (8,), jnp.float32)
        _validS = jnp.arange(128)[None, :] < _lenS[:, None]
        _validS2 = jnp.arange(128)[None, :] < _lenS2[:, None]
        _causal = jnp.tril(jnp.ones((128, 128), dtype=bool))
        mask_Bx4096x4096_ik1 = jnp.where(jnp.ones((8, 512, 512), dtype=bool), 1, 0).astype(jnp.int32)
        return (x, itok_B_6_15, itok_B_3_7, itok_B_1_14, condB_coeff, mask_Bx4096x4096_ik1)
    x, itok_B_6_15, itok_B_3_7, itok_B_1_14, condB_coeff, mask_Bx4096x4096_ik1 = _rec_inputs()

    def _L0_cond_setup():
        import jax, jax.numpy as jnp
        import numpy as np
        B, S, D_IN, D_OUT = (4, 256, 512, 512)
        RANK, MAX_LORAS = (16, 32)
        key = jax.random.key(seed)
        ks = jax.random.split(key, 6)
        x = jax.random.normal(ks[0], (B, S, D_IN), dtype=jnp.float32)
        adapter_ids = jax.random.randint(ks[1], (B,), 0, MAX_LORAS)
        base_weight = jax.random.normal(ks[2], (D_OUT, D_IN), dtype=jnp.float32) * D_IN ** (-0.5)
        base_bias = jax.random.normal(ks[3], (D_OUT,), dtype=jnp.float32) * 0.01
        lora_A_w = jax.random.normal(ks[4], (MAX_LORAS, RANK, D_IN), dtype=jnp.float32) * D_IN ** (-0.5)
        lora_B_w = jax.random.normal(ks[5], (MAX_LORAS, D_OUT, RANK), dtype=jnp.float32) * RANK ** (-0.5)
        return {'x': x, 'adapter_ids': adapter_ids, 'base_weight': base_weight, 'base_bias': base_bias, 'lora_A_w': lora_A_w, 'lora_B_w': lora_B_w}
    _L0_cond_all = _L0_cond_setup()
    _L0_cond_in = {k: v for k, v in _L0_cond_all.items() if k in ('base_weight', 'base_bias', 'lora_A_w', 'lora_B_w')}
    del _L0_cond_all

    def _L1_cond_setup():
        import jax, jax.numpy as jnp
        import numpy as np
        MAX_LORAS, OUT, IN = (8, 512, 512)
        B, S = (4, 256)
        key = jax.random.key(seed)
        k1, k2, k3 = jax.random.split(key, 3)
        x = jax.random.normal(k1, (B, S, IN), dtype=jnp.float32)
        weight = jax.random.normal(k2, (MAX_LORAS, OUT, IN), dtype=jnp.float32) * 0.02
        adapter_ids = jax.random.randint(k3, (B,), 0, MAX_LORAS, dtype=jnp.int32)
        return {'x': x, 'weight': weight, 'adapter_ids': adapter_ids}
    _L1_cond_all = _L1_cond_setup()
    _L1_cond_in = {k: v for k, v in _L1_cond_all.items() if k in ('weight',)}
    del _L1_cond_all

    def _L2_cond_setup():
        import jax, jax.numpy as jnp
        import numpy as np
        B, S, D_IN = (8, 256, 512)
        A, D_OUT = (16, 512)
        key = jax.random.key(seed)
        k1, k2, k3 = jax.random.split(key, 3)
        x = jax.random.normal(k1, (B, S, D_IN), dtype=jnp.float32)
        weight = jax.random.normal(k2, (A, D_OUT, D_IN), dtype=jnp.float32) * 0.02
        adapter_ids = jax.random.randint(k3, (B,), 0, A, dtype=jnp.int64)
        return {'x': x, 'weight': weight, 'adapter_ids': adapter_ids}
    _L2_cond_all = _L2_cond_setup()
    _L2_cond_in = {k: v for k, v in _L2_cond_all.items() if k in ('weight',)}
    del _L2_cond_all

    def _L3_cond_setup():
        import jax, jax.numpy as jnp
        import numpy as np
        B, S, D_IN, D_OUT = (4, 64, 512, 512)
        key = jax.random.key(seed)
        k1, k2, k3, k4, k5 = jax.random.split(key, 5)
        hidden_states = jax.random.normal(k1, (B, S, D_IN), dtype=jnp.float32)
        W = jax.random.normal(k2, (D_OUT, D_IN), dtype=jnp.float32) * 0.02
        b = jax.random.normal(k3, (D_OUT,), dtype=jnp.float32) * 0.02
        coeff = jax.random.normal(k4, (B,), dtype=jnp.float32) * 0.01
        mask = jax.random.randint(k5, (B, D_IN, D_OUT), 0, 2, dtype=jnp.int32)
        return {'hidden_states': hidden_states, 'W': W, 'b': b, 'coeff': coeff, 'mask': mask}
    _L3_cond_all = _L3_cond_setup()
    _L3_cond_in = {k: v for k, v in _L3_cond_all.items() if k in ('W', 'b')}
    del _L3_cond_all
    return {'x': x, 'itok_B_6_15': itok_B_6_15, 'itok_B_3_7': itok_B_3_7, 'itok_B_1_14': itok_B_1_14, 'condB_coeff': condB_coeff, 'mask_Bx4096x4096_ik1': mask_Bx4096x4096_ik1, 'L0_cond_base_weight': _L0_cond_in['base_weight'], 'L0_cond_base_bias': _L0_cond_in['base_bias'], 'L0_cond_lora_A_w': _L0_cond_in['lora_A_w'], 'L0_cond_lora_B_w': _L0_cond_in['lora_B_w'], 'L1_cond_weight': _L1_cond_in['weight'], 'L2_cond_weight': _L2_cond_in['weight'], 'L3_cond_W': _L3_cond_in['W'], 'L3_cond_b': _L3_cond_in['b']}

def reference(x, itok_B_6_15, itok_B_3_7, itok_B_1_14, condB_coeff, mask_Bx4096x4096_ik1, L0_cond_base_weight, L0_cond_base_bias, L0_cond_lora_A_w, L0_cond_lora_B_w, L1_cond_weight, L2_cond_weight, L3_cond_W, L3_cond_b):
    import jax
    import jax.numpy as jnp

    def _L0_cond_ref(x, adapter_ids, base_weight, base_bias, lora_A_w, lora_B_w):
        import jax, jax.numpy as jnp
        import numpy as np
        B, S, D_IN, D_OUT = (4, 256, 512, 512)
        RANK, MAX_LORAS = (16, 32)
        result = jnp.einsum('bsd,od->bso', x, base_weight) + base_bias
        A = lora_A_w[adapter_ids]
        Bw = lora_B_w[adapter_ids]
        h = jnp.einsum('bsd,brd->bsr', x, A)
        lora_out = jnp.einsum('bsr,bor->bso', h, Bw)
        result = result + lora_out
        return result.astype(x.dtype)

    def _L1_cond_ref(x, weight, adapter_ids):
        import jax, jax.numpy as jnp
        import numpy as np
        MAX_LORAS, OUT, IN = (8, 512, 512)
        B, S = (4, 256)
        w = weight[adapter_ids]
        return jnp.einsum('bsi,boi->bso', x, w)

    def _L2_cond_ref(x, weight, adapter_ids):
        import jax, jax.numpy as jnp
        import numpy as np
        B, S, D_IN = (8, 256, 512)
        A, D_OUT = (16, 512)
        w = weight[adapter_ids]
        return jnp.einsum('bij,bkj->bik', x, w)

    def _L3_cond_ref(hidden_states, W, b, coeff, mask):
        import jax, jax.numpy as jnp
        import numpy as np
        B, S, D_IN, D_OUT = (4, 64, 512, 512)
        output = jnp.einsum('bsi,oi->bso', hidden_states, W) + b
        sign = (2 * mask - 1).astype(hidden_states.dtype)
        diff = jnp.einsum('bsi,bio->bso', hidden_states, sign)
        return output + diff * coeff[:, None, None]
    x = x + _L0_cond_ref(x, itok_B_6_15, L0_cond_base_weight, L0_cond_base_bias, L0_cond_lora_A_w, L0_cond_lora_B_w)
    x = x + _L1_cond_ref(x, L1_cond_weight, itok_B_3_7)
    x = x + _L2_cond_ref(x, L2_cond_weight, itok_B_1_14)
    x = x + _L3_cond_ref(x, L3_cond_W, L3_cond_b, condB_coeff, mask_Bx4096x4096_ik1)
    return x

_drawn_inputs = setup_inputs


def setup_inputs(seed=0):
    import zlib

    import numpy as np

    out = dict(_drawn_inputs(seed))
    spreads = {}
    factors = {'L0_cond_base_bias': 8.0, 'L3_cond_b': 7.066}
    for name, (base, spread) in spreads.items():
        noise = np.random.default_rng([zlib.crc32(name.encode()), seed]).standard_normal(out[name].shape)
        drawn = base * np.exp(spread * noise) if base else spread * noise
        out[name] = jnp.asarray(drawn.astype(out[name].dtype))
    for name, factor in factors.items():
        out[name] = (out[name] * factor).astype(out[name].dtype)
    return out
```

```python
from contextlib import ExitStack

import concourse.bass as bass
from concourse import mybir

ALU = mybir.AluOpType
ACT = mybir.ActivationFunctionType
F32 = mybir.dt.float32
F32R = mybir.dt.float32r
I32 = mybir.dt.int32

P = 128
Q = 32


def adapter_chain(nc, x, ids_lora, ids_w1, ids_w2, coeff, mask, base_w, base_b, lora_a, lora_b, w1, w2, w3, b3, out):
    NB, S, D = x.shape
    C = D // P
    R = lora_a.shape[1]
    KB = D // Q
    assert S == P and D == P * C and 2 * R == Q and R * C <= P

    ctx = ExitStack()
    with ctx:
        def sb(name, shape, dt=F32):
            return ctx.enter_context(nc.sbuf_tensor(name, shape, dt))

        def ps(name, shape):
            return ctx.enter_context(nc.psum_tensor(name, shape, F32))

        def sem(name):
            return ctx.enter_context(nc.semaphore(name))

        ident = sb("ident", [P, P])
        ids = sb("ids", [1, 3 * NB], I32)
        coeff_all = sb("coeff_all", [P, NB])
        bias_rows = sb("bias_rows", [2, D])
        bias_hi = sb("bias_hi", [2, D], F32R)
        bias_lo = sb("bias_lo", [2, D], F32R)
        ones2 = sb("ones2", [2, P], F32R)
        bias3 = sb("bias3", [2, D], F32R)
        base_raw = sb("base_raw", [P, C, D])
        w3_raw = sb("w3_raw", [P, C, D])
        base_hi = sb("base_hi", [P, C, D], F32R)
        base_lo = sb("base_lo", [P, C, D], F32R)
        w3_hi = sb("w3_hi", [P, C, D], F32R)
        w3_lo = sb("w3_lo", [P, C, D], F32R)
        w1_raw = sb("w1_raw", [P, KB, P])
        w2_raw = sb("w2_raw", [P, KB, P])
        w1_t = sb("w1_t", [P, C, D])
        w2_t = sb("w2_t", [P, C, D])
        w1_hi = sb("w1_hi", [P, C, D], F32R)
        w1_lo = sb("w1_lo", [P, C, D], F32R)
        w2_hi = sb("w2_hi", [P, C, D], F32R)
        w2_lo = sb("w2_lo", [P, C, D], F32R)
        mask_raw = sb("mask_raw", [P, C * D], I32)
        sign = sb("sign", [P, C, D], F32R)
        a_raw = sb("a_raw", [R, D])
        lora_at = sb("lora_at", [P, C, 3, 2 * R], F32R)
        b_raw = sb("b_raw", [3 * Q, KB, R])
        b_t = sb("b_t", [3 * Q, D])
        h_stack = sb("h_stack", [P, S], F32R)
        b_stack = sb("b_stack", [P, D], F32R)
        x_n = [sb(f"x{l}_n", [P, D]) for l in range(4)]
        x_hi = [sb(f"x{l}_hi", [P, C, S], F32R) for l in range(4)]
        x_lo = [sb(f"x{l}_lo", [P, C, S], F32R) for l in range(4)]
        diff = sb("diff", [P, D])
        y_n = sb("y_n", [P, D])

        ps_31 = ps("ps_31", [P, D])
        ps_sign = ps("ps_sign", [P, D])
        ps_20 = ps("ps_20", [P, D])
        ps_xt = [ps(f"ps_xt{k}", [P, C, S]) for k in range(2)]
        ps_lora = ps("ps_lora", [P, 512])
        ps_wt = [ps(f"ps_wt{k}", [P, C, P]) for k in range(2)]
        ps_h = ps_lora[0:3 * 2 * R, 0:S]
        ps_at = ps_lora[:, S:S + C * R].rearrange("p (c r) -> p c r", c=C)

        ids_ld = sem("ids_ld")
        coeff_ld = sem("coeff_ld")
        bias_ld = sem("bias_ld")
        bias_put = [sem(f"bias_put{k}") for k in range(2)]
        base_ld = [sem(f"base_ld{k}") for k in range(C)]
        w3_ld = sem("w3_ld")
        x_ld = sem("x_ld")
        a_ld = sem("a_ld")
        b_ld = sem("b_ld")
        w1_ld = sem("w1_ld")
        w2_ld = sem("w2_ld")
        mask_ld = sem("mask_ld")
        y_st = sem("y_st")
        ident_zero = sem("ident_zero")
        ident_ok = sem("ident_ok")
        ones_ok = sem("ones_ok")
        bias_hi_ok = sem("bias_hi_ok")
        bias_lo_ok = sem("bias_lo_ok")
        diag_ok = sem("diag_ok")
        shared_tp = sem("shared_tp")
        shared_hi = sem("shared_hi")
        shared_lo = sem("shared_lo")
        x_tp = [sem(f"x{l}_tp") for l in range(4)]
        x_hi_ok = [sem(f"x{l}_hi_ok") for l in range(4)]
        x_lo_ok = [sem(f"x{l}_lo_ok") for l in range(4)]
        x_ok = [None] + [sem(f"x{l}_ok") for l in range(1, 4)]
        mm = [sem(f"mm{l}") for l in range(4)]
        mm_sign = sem("mm_sign")
        a_tp = sem("a_tp")
        a_hi_ok = sem("a_hi_ok")
        a_lo_ok = sem("a_lo_ok")
        h_mm = sem("h_mm")
        h_hi_ok = sem("h_hi_ok")
        h_lo_ok = sem("h_lo_ok")
        b_tp = sem("b_tp")
        b_hi_ok = sem("b_hi_ok")
        b_lo_ok = sem("b_lo_ok")
        w1_tp = sem("w1_tp")
        w2_tp = sem("w2_tp")
        w1_hi_ok = sem("w1_hi_ok")
        w2_hi_ok = sem("w2_hi_ok")
        w1_lo_ok = sem("w1_lo_ok")
        w2_lo_ok = sem("w2_lo_ok")
        sign_ok = sem("sign_ok")
        diff_ok = sem("diff_ok")
        y_ok = sem("y_ok")

        LAST = NB + 3
        LOOP = (4, NB)

        def run_steps(eng, step):
            for t in range(LOOP[0]):
                step(t, [0 <= t - l < NB for l in range(4)])
            with eng.Fori(*LOOP) as t:
                step(t, [True] * 4)
            for t in range(LOOP[1], LAST):
                step(t, [0 <= t - l < NB for l in range(4)])

        def after(eng, s, n):
            if not isinstance(n, int) or n > 0:
                eng.wait_ge(s, n)

        halves = [(h * C // 2, (h + 1) * C // 2) for h in range(2)]
        WARM_UP = 8
        block = ctx.enter_context(nc.Block())

        @block.sync
        def _(sp):
            sp.dma_start(x_n[0][:], x[0]).then_inc(x_ld, 16)
            for k in range(C):
                sp.dma_start(base_raw[:, k, :], base_w[k * P:(k + 1) * P, :]).then_inc(base_ld[k], 16)
            sp.wait_ge(ids_ld, 3 * 16)

            def load_adapter(dst, weights, k, t, s):
                i = sp.value_load(ids[0:1, bass.ds(t + k * NB, 1)], min_val=0, max_val=weights.shape[0] - 1)
                for q in range(P // Q):
                    src = weights[bass.ds(i, 1), :, q * P:(q + 1) * P]
                    sp.dma_start(dst[q * Q:(q + 1) * Q], src.rearrange("a (k r) i -> (a r) k i", r=Q)).then_inc(s, 16)

            def step(t, on):
                if on[0]:
                    if not isinstance(t, int) or t > 0:
                        sp.wait_ge(x_tp[0], t)
                        sp.dma_start(x_n[0][:], x[bass.ds(t, 1)].rearrange("a s d -> (a s) d")).then_inc(x_ld, 16)
                    i = sp.value_load(ids[0:1, bass.ds(t, 1)], min_val=0, max_val=lora_a.shape[0] - 1)
                    after(sp, a_tp, t)
                    sp.dma_start(a_raw[:], lora_a[bass.ds(i, 1)].rearrange("a r d -> (a r) d")).then_inc(a_ld, 16)
                    after(sp, b_tp, t)
                    for q in range(3):
                        sp.dma_start(b_raw[q * Q:(q + 1) * Q],
                                     lora_b[bass.ds(i, 1)].rearrange("a (p k) r -> (a p) k r", k=KB)).then_inc(b_ld, 16)
                    after(sp, w1_tp, t * C)
                    load_adapter(w1_raw, w1, 1, t, w1_ld)
                    after(sp, w2_tp, t * C)
                    load_adapter(w2_raw, w2, 2, t, w2_ld)
                    if isinstance(t, int) and t == 0:
                        sp.dma_start(w3_raw[:], w3.rearrange("(k p) i -> p k i", p=P)).then_inc(w3_ld, 16)
                if on[3]:
                    sp.wait_ge(y_ok, t - 2)
                    sp.dma_start(out[bass.ds(t - 3, 1)].rearrange("a s d -> (a s) d"), y_n[:]).then_inc(y_st, 16)
                if on[1]:
                    after(sp, sign_ok, t - 1)
                    sp.dma_start(mask_raw[:], mask[bass.ds(t - 1, 1)].rearrange("a (p c) o -> (a p) (c o)", c=C)).then_inc(mask_ld, 16)

            run_steps(sp, step)
            sp.wait_ge(y_st, 16 * NB)

        @block.gpsimd
        def _(pool):
            for k, v in enumerate((base_b, b3)):
                pool.dma_start(bias_rows[k:k + 1], v.rearrange("(a b) -> a b", a=1)).then_inc(bias_ld, 16)
            nc.gpsimd.memset(ident[:], 0.0).then_inc(ident_zero, 1)
            pool.wait_ge(ident_zero, 1)
            nc.gpsimd.affine_select(out=ident[:], in_=ident[:], compare_op=ALU.not_equal, fill=1.0, base=0,
                                    pattern=[[-1, P]], channel_multiplier=1).then_inc(ident_ok, 1)
            pool.wait_ge(ident_ok, 1)
            nc.gpsimd.memset(ones2[:].bitcast(F32), 1.0).then_inc(ones_ok, 1)
            pool.wait_ge(ones_ok, 1)
            nc.gpsimd.memset(h_stack[3 * Q:P].bitcast(F32), 1.0).then_inc(ones_ok, 1)
            pool.wait_ge(ones_ok, 2)
            pool.dma_start(coeff_all[:], coeff.rearrange("(a b) -> a b", a=1).broadcast_to([P, NB])).then_inc(coeff_ld, 16)
            pool.wait_ge(bias_lo_ok, 1)
            for k, rows in enumerate((b_stack[3 * Q:3 * Q + 2], bias3[:])):
                for n, part in enumerate((bias_hi, bias_lo)):
                    pool.dma_start(rows[n:n + 1].bitcast(F32), part[k:k + 1].bitcast(F32)).then_inc(bias_put[k], 16)

            def step(t, on):
                if on[0]:
                    for h, (a, b) in enumerate(halves):
                        pool.wait_ge(w1_hi_ok, 2 * t + h + 1)
                        nc.gpsimd.tensor_tensor(w1_lo[:, a:b], w1_t[:, a:b], w1_hi[:, a:b].bitcast(F32),
                                                ALU.subtract).then_inc(w1_lo_ok, 1)

            run_steps(pool, step)

        @block.scalar
        def _(act):
            for k, v in enumerate((ids_lora, ids_w1, ids_w2)):
                act.dma_start(ids[:, k * NB:(k + 1) * NB], v.rearrange("(a b) -> a b", a=1)).then_inc(ids_ld, 16)

            def shared_round(dst, n):
                for k in range(C):
                    act.wait_ge(shared_tp, n + k + 1)
                    nc.scalar.activation(dst[:, :, k * P:(k + 1) * P], ps_wt[k % 2][:], ACT.Copy).then_inc(shared_hi, 1)

            def x_round(l, b):
                act.wait_ge(x_tp[l], b + 1)
                after(act, mm[l], b)
                nc.scalar.activation(x_hi[l][:], ps_xt[1 - l % 2][:], ACT.Copy).then_inc(x_hi_ok[l], 1)

            def w_round(dst, src, b, tp, used, ok):
                for h, (a, e) in enumerate(halves):
                    act.wait_ge(tp, C * b + e)
                    if h == 0:
                        after(act, used, b)
                    nc.scalar.activation(dst[:, a:e], src[:, a:e], ACT.Copy).then_inc(ok, 1)

            act.wait_ge(bias_ld, 2 * 16)
            nc.scalar.activation(bias_hi[:], bias_rows[:], ACT.Copy).then_inc(bias_hi_ok, 1)
            x_round(0, 0)
            shared_round(base_hi, 0)
            act.wait_ge(coeff_ld, 16)

            def step(t, on):
                if on[1]:
                    x_round(1, t - 1)
                if on[3]:
                    act.wait_ge(mm_sign, t - 2)
                    after(act, y_ok, t - 3)
                    nc.scalar.activation(diff[:], ps_sign[:], ACT.Copy,
                                         scale=coeff_all[:, bass.ds(t - 3, 1)]).then_inc(diff_ok, 1)
                if on[2]:
                    act.wait_ge(mask_ld, 16 * (t - 1))
                    after(act, mm_sign, t - 2)
                    nc.scalar.activation(sign[:].rearrange("p c o -> p (c o)"), mask_raw[:], ACT.Copy,
                                         scale=2.0, bias=-1.0).then_inc(sign_ok, 1)
                if on[0]:
                    if not isinstance(t, int) or t > 0:
                        x_round(0, t)
                    act.wait_ge(a_tp, t + 1)
                    after(act, h_mm, t)
                    nc.scalar.activation(lora_at[:, :, :, 0:R], ps_at.unsqueeze(2).broadcast_to([P, C, 3, R]),
                                         ACT.Copy).then_inc(a_hi_ok, 1)
                if on[1]:
                    w_round(w2_hi, w2_t, t - 1, w2_tp, mm[2], w2_hi_ok)
                if on[2]:
                    x_round(3, t - 2)
                if on[0]:
                    act.wait_ge(b_tp, t + 1)
                    after(act, mm[0], t)
                    nc.scalar.activation(b_stack[0:3 * Q], b_t[:], ACT.Copy).then_inc(b_hi_ok, 1)
                    act.wait_ge(h_mm, t + 1)
                    nc.scalar.activation(h_stack[0:3 * Q], ps_h, ACT.Copy).then_inc(h_hi_ok, 1)
                    w_round(w1_hi, w1_t, t, w1_tp, mm[1], w1_hi_ok)
                    act.wait_ge(mm[0], t + 1)
                    after(act, x_ok[2], t)
                    nc.scalar.activation(x_n[1][:], ps_20[:], ACT.Copy).then_inc(x_ok[1], 1)
                if on[1]:
                    x_round(2, t - 1)
                if isinstance(t, int) and t == 1:
                    shared_round(w3_hi, C)

            run_steps(act, step)

        @block.vector
        def _(dve):
            def shared_diag(raw, k, n):
                v = raw[:, k, k * P:(k + 1) * P]
                nc.vector.tensor_tensor(v, v, ident[:], ALU.add).then_inc(diag_ok, 1)

            def shared_rest(lo, hi, n):
                for k in range(C):
                    dve.wait_ge(shared_hi, n + k + 1)
                    nc.vector.tensor_tensor(lo[:, :, k * P:(k + 1) * P], ps_wt[k % 2][:],
                                            hi[:, :, k * P:(k + 1) * P].bitcast(F32), ALU.subtract).then_inc(shared_lo, 1)

            def x_rest(l, b):
                dve.wait_ge(x_hi_ok[l], b + 1)
                nc.vector.tensor_tensor(x_lo[l][:], ps_xt[1 - l % 2][:], x_hi[l][:].bitcast(F32),
                                        ALU.subtract).then_inc(x_lo_ok[l], 1)

            def w_turn(dst, raw, b, ld, used, tp):
                dve.wait_ge(ld, 16 * (P // Q) * (b + 1))
                after(dve, used, 2 * b)
                for c in range(C):
                    nc.vector.transpose(dst[:, c, :].rearrange("p (k j) -> p k j", j=Q),
                                        raw[:].rearrange("p k (j c) -> p c k j", c=C)[:, c]).then_inc(tp, 1)

            dve.wait_ge(ident_ok, 1)
            for k in range(C):
                dve.wait_ge(base_ld[k], 16)
                shared_diag(base_raw, k, 0)
                if k == 0:
                    dve.wait_ge(bias_hi_ok, 1)
                    nc.vector.tensor_tensor(bias_lo[:], bias_rows[:], bias_hi[:].bitcast(F32), ALU.subtract).then_inc(bias_lo_ok, 1)
                    x_rest(0, 0)
            shared_rest(base_lo, base_hi, 0)

            def step(t, on):
                if on[1]:
                    w_turn(w2_t, w2_raw, t - 1, w2_ld, w2_lo_ok, w2_tp)
                    x_rest(1, t - 1)
                if on[0]:
                    dve.wait_ge(b_ld, 3 * 16 * (t + 1))
                    after(dve, b_lo_ok, t)
                    nc.vector.transpose(b_t[:].rearrange("q (p k) -> q k p", k=KB),
                                        b_raw[:].unsqueeze(2).broadcast_to([3 * Q, KB, 2, R])).then_inc(b_tp, 1)
                if on[3]:
                    dve.wait_ge(diff_ok, t - 2)
                    dve.wait_ge(mm[3], t - 2)
                    after(dve, y_st, 16 * (t - 3))
                    nc.vector.tensor_tensor(y_n[:], ps_31[:], diff[:], ALU.add).then_inc(y_ok, 1)
                if on[2]:
                    dve.wait_ge(mm[2], t - 1)
                    nc.vector.tensor_tensor(x_n[3][:], ps_20[:], x_n[2][:], ALU.add).then_inc(x_ok[3], 1)
                if on[0]:
                    if not isinstance(t, int) or t > 0:
                        x_rest(0, t)
                    dve.wait_ge(a_hi_ok, t + 1)
                    nc.vector.tensor_tensor(lora_at[:, :, :, R:2 * R], ps_at.unsqueeze(2).broadcast_to([P, C, 3, R]),
                                            lora_at[:, :, :, 0:R].bitcast(F32), ALU.subtract).then_inc(a_lo_ok, 1)
                    w_turn(w1_t, w1_raw, t, w1_ld, w1_lo_ok, w1_tp)
                if on[1]:
                    if on[2]:
                        dve.wait_ge(x_ok[3], t - 1)
                    dve.wait_ge(mm[1], t)
                    nc.vector.tensor_tensor(x_n[2][:], ps_31[:], x_n[1][:], ALU.add).then_inc(x_ok[2], 1)
                if on[2]:
                    x_rest(3, t - 2)
                if on[0]:
                    dve.wait_ge(b_hi_ok, t + 1)
                    nc.vector.tensor_tensor(b_stack[2 * Q:3 * Q], b_t[2 * Q:3 * Q], b_stack[2 * Q:3 * Q].bitcast(F32),
                                            ALU.subtract).then_inc(b_lo_ok, 1)
                    dve.wait_ge(h_hi_ok, t + 1)
                    nc.vector.tensor_tensor(h_stack[Q:2 * Q], ps_h[Q:2 * Q], h_stack[Q:2 * Q].bitcast(F32),
                                            ALU.subtract).then_inc(h_lo_ok, 1)
                if on[1]:
                    for h, (a, e) in enumerate(halves):
                        dve.wait_ge(w2_hi_ok, 2 * (t - 1) + h + 1)
                        nc.vector.tensor_tensor(w2_lo[:, a:e], w2_t[:, a:e], w2_hi[:, a:e].bitcast(F32),
                                                ALU.subtract).then_inc(w2_lo_ok, 1)
                    x_rest(2, t - 1)
                if isinstance(t, int) and t == 1:
                    dve.wait_ge(w3_ld, 16)
                    for k in range(C):
                        shared_diag(w3_raw, k, C)
                    shared_rest(w3_lo, w3_hi, C)

            run_steps(dve, step)

        @block.tensor
        def _(pe):
            def shared_turn(raw, n):
                for k in range(C):
                    pe.wait_ge(diag_ok, n + k + 1)
                    after(pe, shared_lo, n + k - 1)
                    for c in range(C):
                        last = nc.tensor.transpose(ps_wt[k % 2][:, c, :], raw[:, k, c:D:C], ident[:])
                    last.then_inc(shared_tp, 1)

            def x_turn(l):
                for c in range(C):
                    last = nc.tensor.transpose(ps_xt[1 - l % 2][:, c, :], x_n[l][:, c:D:C], ident[:])
                last.then_inc(x_tp[l], 1)

            def products(dst, l, hi, lo, closes=True):
                for c in range(C):
                    nc.tensor.matmul(dst, x_hi[l][:, c], hi[:, c], start=(c == 0), stop=False)
                    nc.tensor.matmul(dst, x_hi[l][:, c], lo[:, c], start=False, stop=False)
                    last = nc.tensor.matmul(dst, x_lo[l][:, c], hi[:, c], start=False, stop=(closes and c == C - 1))
                return last

            pe.wait_ge(ident_ok, 1)
            for k in range(WARM_UP):
                nc.tensor.transpose(ps_sign[:, 0:P], ident[:], ident[:])
            pe.wait_ge(x_ld, 16)
            x_turn(0)
            shared_turn(base_raw, 0)

            def step(t, on):
                if on[3]:
                    pe.wait_ge(x_lo_ok[3], t - 2)
                    pe.wait_ge(sign_ok, t - 2)
                    after(pe, diff_ok, t - 3)
                    for c in range(C):
                        nc.tensor.matmul(ps_sign[:], x_hi[3][:, c], sign[:, c], start=(c == 0), stop=False)
                        last = nc.tensor.matmul(ps_sign[:], x_lo[3][:, c], sign[:, c], start=False, stop=(c == C - 1))
                    last.then_inc(mm_sign, 1)
                    if isinstance(t, int) and t == 3:
                        pe.wait_ge(shared_lo, 2 * C)
                        pe.wait_ge(bias_put[1], 2 * 16)
                    products(ps_31[:], 3, w3_hi, w3_lo, closes=False)
                    nc.tensor.matmul(ps_31[:], ones2[:], bias3[:], start=False, stop=True).then_inc(mm[3], 1)
                if on[1]:
                    pe.wait_ge(x_ok[1], t)
                    x_turn(1)
                if on[2]:
                    pe.wait_ge(x_lo_ok[2], t - 1)
                    pe.wait_ge(w2_lo_ok, 2 * (t - 1))
                    products(ps_20[:], 2, w2_hi, w2_lo).then_inc(mm[2], 1)
                if on[0]:
                    pe.wait_ge(a_ld, 16 * (t + 1))
                    pe.wait_ge(x_ld, 16 * (t + 1))
                    if isinstance(t, int) and t == 0:
                        nc.tensor.transpose(ps_sign[:, 0:P], ident[:], ident[:])
                    else:
                        x_turn(0)
                    for c in range(C):
                        last = nc.tensor.transpose(ps_at[:, c, :], a_raw[:, c:D:C], ident[0:R, 0:R])
                    last.then_inc(a_tp, 1)
                if on[1]:
                    pe.wait_ge(x_lo_ok[1], t)
                    pe.wait_ge(w1_lo_ok, 2 * t)
                    if on[3]:
                        pe.wait_ge(y_ok, t - 2)
                    products(ps_31[:], 1, w1_hi, w1_lo).then_inc(mm[1], 1)
                if on[2]:
                    pe.wait_ge(x_ok[3], t - 1)
                    x_turn(3)
                if on[0]:
                    pe.wait_ge(x_lo_ok[0], t + 1)
                    pe.wait_ge(a_lo_ok, t + 1)
                    for c in range(C):
                        a = lora_at[:, c].rearrange("p n r -> p (n r)")
                        nc.tensor.matmul(ps_h, a, x_hi[0][:, c], start=(c == 0), stop=False)
                        last = nc.tensor.matmul(ps_h, a, x_lo[0][:, c], start=False, stop=(c == C - 1))
                    last.then_inc(h_mm, 1)
                    if isinstance(t, int) and t == 0:
                        pe.wait_ge(shared_lo, C)
                        pe.wait_ge(ones_ok, 2)
                    products(ps_20[:], 0, base_hi, base_lo, closes=False)
                    pe.wait_ge(h_lo_ok, t + 1)
                    pe.wait_ge(b_lo_ok, t + 1)
                    if isinstance(t, int) and t == 0:
                        pe.wait_ge(bias_put[0], 2 * 16)
                    nc.tensor.matmul(ps_20[:], h_stack[0:3 * Q + 2], b_stack[0:3 * Q + 2],
                                     start=False, stop=True).then_inc(mm[0], 1)
                if on[1]:
                    pe.wait_ge(x_ok[2], t)
                    x_turn(2)
                if isinstance(t, int) and t == 1:
                    shared_turn(w3_raw, C)

            run_steps(pe, step)


_INS = ['x', 'itok_B_6_15', 'itok_B_3_7', 'itok_B_1_14', 'condB_coeff', 'mask_Bx4096x4096_ik1',
        'L0_cond_base_weight', 'L0_cond_base_bias', 'L0_cond_lora_A_w', 'L0_cond_lora_B_w',
        'L1_cond_weight', 'L2_cond_weight', 'L3_cond_W', 'L3_cond_b']


def kernel(**inputs):
    import numpy as _np
    import concourse.bacc as _bacc
    from concourse import mybir as _mybir
    from concourse.bass_utils import run_bass_kernel_spmd as _run

    nc = _bacc.Bacc("TRN2", target_bir_lowering=False, num_devices=1)
    arrays, args = {}, []
    for name in _INS:
        a = _np.ascontiguousarray(inputs[name])
        arrays[f"in_{name}_dram"] = a
        args.append(nc.dram_tensor(f"in_{name}_dram", a.shape, _mybir.dt.from_np(a.dtype), kind="ExternalInput").ap())
    shape = inputs['x'].shape
    args.append(nc.dram_tensor("out_0_dram", shape, _mybir.dt.from_np(_np.dtype('float32')), kind="ExternalOutput").ap())
    adapter_chain(nc, *args)
    r = _run(nc, [arrays], core_ids=[0])
    return r.results[0]["out_0_dram"]
```

```python
from contextlib import ExitStack

import concourse.bass as bass
from concourse import mybir

ALU = mybir.AluOpType
ACT = mybir.ActivationFunctionType
F32 = mybir.dt.float32
F32R = mybir.dt.float32r
I32 = mybir.dt.int32

P = 128
Q = 32


def adapter_chain(nc, x, ids_lora, ids_w1, ids_w2, coeff, mask, base_w, base_b, lora_a, lora_b, w1, w2, w3, b3, out):
    NB, S, D = x.shape
    C = D // P
    R = lora_a.shape[1]
    KB = D // Q
    assert S == P and D == P * C and 2 * R == Q and R * C <= P

    ctx = ExitStack()
    with ctx:
        def sb(name, shape, dt=F32):
            return ctx.enter_context(nc.sbuf_tensor(name, shape, dt))

        def ps(name, shape):
            return ctx.enter_context(nc.psum_tensor(name, shape, F32))

        def sem(name):
            return ctx.enter_context(nc.semaphore(name))

        ident = sb("ident", [P, P])
        ids = sb("ids", [1, 3 * NB], I32)
        coeff_all = sb("coeff_all", [P, NB])
        bias_rows = sb("bias_rows", [2, D])
        bias_hi = sb("bias_hi", [2, D], F32R)
        bias_lo = sb("bias_lo", [2, D], F32R)
        ones2 = sb("ones2", [2, P], F32R)
        bias3 = sb("bias3", [2, D], F32R)
        base_raw = sb("base_raw", [P, C, D])
        w3_raw = sb("w3_raw", [P, C, D])
        base_hi = sb("base_hi", [P, C, D], F32R)
        base_lo = sb("base_lo", [P, C, D], F32R)
        w3_hi = sb("w3_hi", [P, C, D], F32R)
        w3_lo = sb("w3_lo", [P, C, D], F32R)
        w1_raw = sb("w1_raw", [P, KB, P])
        w2_raw = sb("w2_raw", [P, KB, P])
        w1_t = sb("w1_t", [P, C, D])
        w2_t = sb("w2_t", [P, C, D])
        w1_hi = sb("w1_hi", [P, C, D], F32R)
        w1_lo = sb("w1_lo", [P, C, D], F32R)
        w2_hi = sb("w2_hi", [P, C, D], F32R)
        w2_lo = sb("w2_lo", [P, C, D], F32R)
        mask_raw = sb("mask_raw", [P, C * D], I32)
        sign = sb("sign", [P, C, D], F32R)
        a_raw = sb("a_raw", [R, D])
        lora_at = sb("lora_at", [P, C, 3, 2 * R], F32R)
        b_raw = sb("b_raw", [3 * Q, KB, R])
        b_t = sb("b_t", [3 * Q, D])
        h_stack = sb("h_stack", [P, S], F32R)
        b_stack = sb("b_stack", [P, D], F32R)
        x_n = [sb(f"x{l}_n", [P, D]) for l in range(4)]
        x_hi = [sb(f"x{l}_hi", [P, C, S], F32R) for l in range(4)]
        x_lo = [sb(f"x{l}_lo", [P, C, S], F32R) for l in range(4)]
        diff = sb("diff", [P, D])
        y_n = sb("y_n", [P, D])

        ps_31 = ps("ps_31", [P, D])
        ps_sign = ps("ps_sign", [P, D])
        ps_20 = ps("ps_20", [P, D])
        ps_xt = [ps(f"ps_xt{k}", [P, C, S]) for k in range(2)]
        ps_lora = ps("ps_lora", [P, 512])
        ps_wt = [ps(f"ps_wt{k}", [P, C, P]) for k in range(2)]
        ps_h = ps_lora[0:3 * 2 * R, 0:S]
        ps_at = ps_lora[:, S:S + C * R].rearrange("p (c r) -> p c r", c=C)

        ids_ld = [sem(f"ids{k}_ld") for k in range(3)]
        coeff_ld = sem("coeff_ld")
        bias_ld = sem("bias_ld")
        bias_put = [sem(f"bias_put{k}") for k in range(2)]
        base_ld = [sem(f"base_ld{k}") for k in range(C)]
        first_ld = [[sem(f"first{n}_ld{k}") for k in range(C)] for n in (1, 2, 3)]
        x_ld = sem("x_ld")
        x_spare_ld = sem("x_spare_ld")
        a_ld = sem("a_ld")
        b_ld = sem("b_ld")
        w1_ld = sem("w1_ld")
        w2_ld = sem("w2_ld")
        mask_ld = sem("mask_ld")
        y_st = sem("y_st")
        ident_zero = sem("ident_zero")
        ident_ok = sem("ident_ok")
        ones_ok = sem("ones_ok")
        bias_hi_ok = sem("bias_hi_ok")
        bias_lo_ok = sem("bias_lo_ok")
        base_diag_ok = sem("base_diag_ok")
        w3_diag_ok = sem("w3_diag_ok")
        unit_tp = sem("unit_tp")
        unit_hi = sem("unit_hi")
        unit_lo = sem("unit_lo")
        x_tp = [sem(f"x{l}_tp") for l in range(4)]
        x_hi_ok = [sem(f"x{l}_hi_ok") for l in range(4)]
        x_lo_ok = [sem(f"x{l}_lo_ok") for l in range(4)]
        x_ok = [None] + [sem(f"x{l}_ok") for l in range(1, 4)]
        mm = [sem(f"mm{l}") for l in range(4)]
        mm_sign = sem("mm_sign")
        a_tp = sem("a_tp")
        a_hi_ok = sem("a_hi_ok")
        a_lo_ok = sem("a_lo_ok")
        h_mm = sem("h_mm")
        h_hi_ok = sem("h_hi_ok")
        h_lo_ok = sem("h_lo_ok")
        b_tp = sem("b_tp")
        b_hi_ok = sem("b_hi_ok")
        b_lo_ok = sem("b_lo_ok")
        w1_tp = sem("w1_tp")
        w2_tp = sem("w2_tp")
        w1_hi_ok = sem("w1_hi_ok")
        w2_hi_ok = sem("w2_hi_ok")
        w1_lo_ok = sem("w1_lo_ok")
        w2_lo_ok = sem("w2_lo_ok")
        sign_ok = sem("sign_ok")
        diff_ok = sem("diff_ok")
        y_ok = sem("y_ok")

        LOOP = (4, NB)
        BASE, W1, W2, W3 = range(0, 4 * C, C)
        WARM_UP = 12

        def before(eng, s, n):
            if not isinstance(n, int) or n > 0:
                eng.wait_ge(s, n)

        def spare(l, b):
            return 3 - l if isinstance(b, int) and (l, b) in ((0, 1), (3, NB - 1)) else l

        halves = [(h * C // 2, (h + 1) * C // 2) for h in range(2)]

        def unit_bank(n):
            units = [ps_wt[0], ps_wt[1], ps_sign, ps_31]
            if n >= W2:
                units = [ps_wt[0], ps_wt[1], ps_sign] if n < W3 else [ps_wt[0], ps_sign]
            bank = units[n % C % len(units)]
            return bank[:] if bank in ps_wt else bank[:].rearrange("p (c o) -> p c o", c=C)

        def unit_after(n):
            return n - C + 1 if n < W2 else (max(W2, n - 2) if n < W3 else max(W3, n - 1))

        def layer0_bank(b):
            return ps_wt[1][:].rearrange("p c o -> p (c o)") if isinstance(b, int) and b == 2 else ps_20[:]

        def as_loaded(raw):
            return raw[:].rearrange("p k j -> p (k j)").rearrange("p (n i) -> p n i", i=D)

        block = ctx.enter_context(nc.Block())

        @block.sync
        def _(sp):
            def index(k, b, count):
                return sp.value_load(ids[0:1, bass.ds(b + k * NB, 1)], min_val=0, max_val=count - 1)

            def load_x(b):
                before(sp, x_tp[0], b)
                sp.dma_start(x_n[0][:], x[bass.ds(b, 1)].rearrange("a s d -> (a s) d")).then_inc(x_ld, 16)

            def load_lora(b):
                i = index(0, b, lora_a.shape[0])
                before(sp, a_tp, b)
                sp.dma_start(a_raw[:], lora_a[bass.ds(i, 1)].rearrange("a r d -> (a r) d")).then_inc(a_ld, 16)
                before(sp, b_tp, b)
                for q in range(3):
                    sp.dma_start(b_raw[q * Q:(q + 1) * Q],
                                 lora_b[bass.ds(i, 1)].rearrange("a (p k) r -> (a p) k r", k=KB)).then_inc(b_ld, 16)

            def load_rows(dst, src, k, s):
                sp.dma_start(dst[:, k, :], src[k * P:(k + 1) * P, :]).then_inc(s[k], 16)

            def load_first(dst, weights, n, units):
                i = index(n, 0, weights.shape[0])
                for k in units:
                    src = weights[bass.ds(i, 1), k * P:(k + 1) * P, :].rearrange("a p i -> (a p) i")
                    sp.dma_start(as_loaded(dst)[:, k, :], src).then_inc(first_ld[n - 1][k], 16)

            def load_adapter(dst, weights, k, b, tp, s):
                i = index(k, b, weights.shape[0])
                if isinstance(b, int) and b == 1:
                    sp.wait_ge(unit_tp, (W1, W2)[k - 1] + C)
                else:
                    sp.wait_ge(tp, (b - 1) * C)
                for q in range(P // Q):
                    src = weights[bass.ds(i, 1), :, q * P:(q + 1) * P]
                    sp.dma_start(dst[q * Q:(q + 1) * Q], src.rearrange("a (k r) i -> (a r) k i", r=Q)).then_inc(s, 16)

            def load_mask(b):
                before(sp, sign_ok, b)
                sp.dma_start(mask_raw[:], mask[bass.ds(b, 1)].rearrange("a (p c) o -> (a p) (c o)", c=C)).then_inc(mask_ld, 16)

            def store_y(b):
                sp.wait_ge(y_ok, b + 1)
                sp.dma_start(out[bass.ds(b, 1)].rearrange("a s d -> (a s) d"), y_n[:]).then_inc(y_st, 16)

            def put_bias(k, rows):
                sp.wait_ge(bias_lo_ok, 1)
                for n, part in enumerate((bias_hi, bias_lo)):
                    sp.dma_start(rows[n:n + 1].bitcast(F32), part[k:k + 1].bitcast(F32)).then_inc(bias_put[k], 16)

            def step(t):
                load_x(t)
                load_lora(t)
                load_adapter(w1_raw, w1, 1, t, w1_tp, w1_ld)
                load_adapter(w2_raw, w2, 2, t, w2_tp, w2_ld)
                store_y(t - 3)
                load_mask(t - 1)

            load_x(0)
            for k in range(C):
                load_rows(base_raw, base_w, k, base_ld)
            sp.wait_ge(ids_ld[0], 16)
            load_lora(0)
            sp.wait_ge(ids_ld[1], 16)
            load_first(w1_raw, w1, 1, range(0, 2))
            sp.dma_start(x_n[spare(0, 1)][:], x[1]).then_inc(x_spare_ld, 16)
            put_bias(0, b_stack[3 * Q:3 * Q + 2])
            load_first(w1_raw, w1, 1, range(2, C))
            load_lora(1)
            sp.wait_ge(ids_ld[2], 16)
            load_first(w2_raw, w2, 2, range(0, C // 2))
            load_x(2)
            load_first(w2_raw, w2, 2, range(C // 2, C))
            load_lora(2)
            load_adapter(w1_raw, w1, 1, 1, w1_tp, w1_ld)
            for k in range(C):
                load_rows(w3_raw, w3, k, first_ld[2])
            put_bias(1, bias3[:])
            load_adapter(w2_raw, w2, 2, 1, w2_tp, w2_ld)
            load_mask(0)
            load_adapter(w1_raw, w1, 1, 2, w1_tp, w1_ld)
            load_adapter(w2_raw, w2, 2, 2, w2_tp, w2_ld)
            load_mask(1)
            step(3)
            with sp.Fori(*LOOP) as t:
                step(t)
            store_y(NB - 3)
            load_mask(NB - 1)
            store_y(NB - 2)
            store_y(NB - 1)
            sp.wait_ge(y_st, 16 * NB)

        @block.gpsimd
        def _(pool):
            nc.gpsimd.memset(ident[:], 0.0).then_inc(ident_zero, 1)
            pool.wait_ge(ident_zero, 1)
            nc.gpsimd.affine_select(out=ident[:], in_=ident[:], compare_op=ALU.not_equal, fill=1.0, base=0,
                                    pattern=[[-1, P]], channel_multiplier=1).then_inc(ident_ok, 1)
            for k, v in enumerate((base_b, b3)):
                pool.dma_start(bias_rows[k:k + 1], v.rearrange("(a b) -> a b", a=1)).then_inc(bias_ld, 16)
            pool.wait_ge(ident_ok, 1)
            nc.gpsimd.memset(ones2[:].bitcast(F32), 1.0).then_inc(ones_ok, 1)
            pool.wait_ge(ones_ok, 1)
            nc.gpsimd.memset(h_stack[3 * Q:P].bitcast(F32), 1.0).then_inc(ones_ok, 1)
            pool.wait_ge(ones_ok, 2)
            pool.dma_start(coeff_all[:], coeff.rearrange("(a b) -> a b", a=1).broadcast_to([P, NB])).then_inc(coeff_ld, 16)

            def add_diag(raw, k, ok):
                v = raw[:, k, k * P:(k + 1) * P]
                nc.gpsimd.tensor_tensor(v, v, ident[:], ALU.add).then_inc(ok, 1)
                pool.wait_ge(ok, k + 1)

            def w1_rest(b, parts):
                for h in parts:
                    a, e = halves[h]
                    pool.wait_ge(w1_hi_ok, 2 * (b - 1) + h + 1)
                    nc.gpsimd.tensor_tensor(w1_lo[:, a:e], w1_t[:, a:e], w1_hi[:, a:e].bitcast(F32),
                                            ALU.subtract).then_inc(w1_lo_ok, 1)

            for k in range(C):
                pool.wait_ge(base_ld[k], 16)
                add_diag(base_raw, k, base_diag_ok)
            for k in range(C):
                pool.wait_ge(first_ld[2][k], 16)
                add_diag(w3_raw, k, w3_diag_ok)
            w1_rest(1, [0])
            w1_rest(2, [0, 1])
            w1_rest(3, [0, 1])
            with pool.Fori(*LOOP) as t:
                w1_rest(t, [0, 1])

        @block.scalar
        def _(act):
            for k, v in enumerate((ids_lora, ids_w1, ids_w2)):
                act.dma_start(ids[:, k * NB:(k + 1) * NB], v.rearrange("(a b) -> a b", a=1)).then_inc(ids_ld[k], 16)

            def units_round(dst, n, units=range(C)):
                for k in units:
                    act.wait_ge(unit_tp, n + k + 1)
                    nc.scalar.activation(dst[:, :, k * P:(k + 1) * P], unit_bank(n + k), ACT.Copy).then_inc(unit_hi, 1)

            def x_round(l, b):
                act.wait_ge(x_tp[l], b + 1)
                if spare(l, b) == l:
                    before(act, mm[l], b)
                nc.scalar.activation(x_hi[spare(l, b)][:], ps_xt[1 - l % 2][:], ACT.Copy).then_inc(x_hi_ok[l], 1)

            def w_round(dst, src, b, tp, used, ok):
                for h, (a, e) in enumerate(halves):
                    act.wait_ge(tp, C * (b - 1) + e)
                    if h == 0:
                        act.wait_ge(used, b)
                    nc.scalar.activation(dst[:, a:e], src[:, a:e], ACT.Copy).then_inc(ok, 1)

            def w1_round(b):
                w_round(w1_hi, w1_t, b, w1_tp, mm[1], w1_hi_ok)

            def w2_round(b):
                w_round(w2_hi, w2_t, b, w2_tp, mm[2], w2_hi_ok)

            def a_round(b):
                act.wait_ge(a_tp, b + 1)
                before(act, h_mm, b)
                nc.scalar.activation(lora_at[:, :, :, 0:R], ps_at.unsqueeze(2).broadcast_to([P, C, 3, R]),
                                     ACT.Copy).then_inc(a_hi_ok, 1)

            def b_round(b):
                act.wait_ge(b_tp, b + 1)
                before(act, mm[0], b)
                nc.scalar.activation(b_stack[0:3 * Q], b_t[:], ACT.Copy).then_inc(b_hi_ok, 1)

            def h_round(b):
                act.wait_ge(h_mm, b + 1)
                nc.scalar.activation(h_stack[0:3 * Q], ps_h, ACT.Copy).then_inc(h_hi_ok, 1)

            def x1_out(b):
                act.wait_ge(mm[0], b + 1)
                before(act, x_ok[2], b)
                nc.scalar.activation(x_n[1][:], layer0_bank(b), ACT.Copy).then_inc(x_ok[1], 1)

            def signs(b):
                act.wait_ge(mask_ld, 16 * (b + 1))
                before(act, mm_sign, b)
                nc.scalar.activation(sign[:].rearrange("p c o -> p (c o)"), mask_raw[:], ACT.Copy,
                                     scale=2.0, bias=-1.0).then_inc(sign_ok, 1)

            def scale_diff(b):
                act.wait_ge(mm_sign, b + 1)
                before(act, y_ok, b)
                nc.scalar.activation(diff[:], ps_sign[:], ACT.Copy,
                                     scale=coeff_all[:, bass.ds(b, 1)]).then_inc(diff_ok, 1)

            def step(t):
                x_round(1, t - 1)
                scale_diff(t - 3)
                signs(t - 2)
                x_round(0, t)
                a_round(t)
                w2_round(t - 1)
                x_round(3, t - 2)
                b_round(t)
                h_round(t)
                w1_round(t)
                x1_out(t)
                x_round(2, t - 1)

            x_round(0, 0)
            act.wait_ge(bias_ld, 2 * 16)
            nc.scalar.activation(bias_hi[:], bias_rows[:], ACT.Copy).then_inc(bias_hi_ok, 1)
            units_round(base_hi, BASE)
            a_round(0)
            b_round(0)
            h_round(0)
            x_round(0, 1)
            x1_out(0)
            units_round(w1_hi, W1)
            a_round(1)
            b_round(1)
            x_round(1, 0)
            h_round(1)
            units_round(w2_hi, W2, range(0, C // 2))
            x_round(0, 2)
            units_round(w2_hi, W2, range(C // 2, C - 1))
            a_round(2)
            units_round(w2_hi, W2, range(C - 1, C))
            b_round(2)
            x1_out(1)
            h_round(2)
            x_round(2, 0)
            x_round(1, 1)
            w1_round(1)
            signs(0)
            units_round(w3_hi, W3, range(0, 2))
            x_round(3, 0)
            units_round(w3_hi, W3, range(2, C))
            x1_out(2)
            w2_round(1)
            x_round(2, 1)
            w1_round(2)
            act.wait_ge(coeff_ld, 16)
            step(3)
            with act.Fori(*LOOP) as t:
                step(t)
            x_round(1, NB - 1)
            scale_diff(NB - 3)
            signs(NB - 2)
            w2_round(NB - 1)
            x_round(3, NB - 2)
            x_round(2, NB - 1)
            scale_diff(NB - 2)
            signs(NB - 1)
            x_round(3, NB - 1)
            scale_diff(NB - 1)

        @block.vector
        def _(dve):
            def units_rest(lo, hi, n, units=range(C)):
                for k in units:
                    dve.wait_ge(unit_hi, n + k + 1)
                    nc.vector.tensor_tensor(lo[:, :, k * P:(k + 1) * P], unit_bank(n + k),
                                            hi[:, :, k * P:(k + 1) * P].bitcast(F32), ALU.subtract).then_inc(unit_lo, 1)

            def x_rest(l, b):
                dve.wait_ge(x_hi_ok[l], b + 1)
                nc.vector.tensor_tensor(x_lo[spare(l, b)][:], ps_xt[1 - l % 2][:], x_hi[spare(l, b)][:].bitcast(F32),
                                        ALU.subtract).then_inc(x_lo_ok[l], 1)

            def w_turn(dst, raw, b, ld, used, tp, chunks=range(C)):
                dve.wait_ge(ld, 16 * (P // Q) * b)
                before(dve, used, 2 * (b - 1))
                for c in chunks:
                    nc.vector.transpose(dst[:, c, :].rearrange("p (k j) -> p k j", j=Q),
                                        raw[:].rearrange("p k (j c) -> p c k j", c=C)[:, c]).then_inc(tp, 1)

            def w1_turn(b, chunks=range(C)):
                w_turn(w1_t, w1_raw, b, w1_ld, w1_lo_ok, w1_tp, chunks)

            def w2_turn(b):
                w_turn(w2_t, w2_raw, b, w2_ld, w2_lo_ok, w2_tp)

            def w_rest(lo, t_, hi, b, hi_ok, lo_ok, parts):
                for h in parts:
                    a, e = halves[h]
                    dve.wait_ge(hi_ok, 2 * (b - 1) + h + 1)
                    nc.vector.tensor_tensor(lo[:, a:e], t_[:, a:e], hi[:, a:e].bitcast(F32), ALU.subtract).then_inc(lo_ok, 1)

            def w2_rest(b):
                w_rest(w2_lo, w2_t, w2_hi, b, w2_hi_ok, w2_lo_ok, [0, 1])

            def a_rest(b):
                dve.wait_ge(a_hi_ok, b + 1)
                nc.vector.tensor_tensor(lora_at[:, :, :, R:2 * R], ps_at.unsqueeze(2).broadcast_to([P, C, 3, R]),
                                        lora_at[:, :, :, 0:R].bitcast(F32), ALU.subtract).then_inc(a_lo_ok, 1)

            def b_turn(b):
                dve.wait_ge(b_ld, 3 * 16 * (b + 1))
                before(dve, b_lo_ok, b)
                nc.vector.transpose(b_t[:].rearrange("q (p k) -> q k p", k=KB),
                                    b_raw[:].unsqueeze(2).broadcast_to([3 * Q, KB, 2, R])).then_inc(b_tp, 1)

            def b_rest(b):
                dve.wait_ge(b_hi_ok, b + 1)
                nc.vector.tensor_tensor(b_stack[2 * Q:3 * Q], b_t[2 * Q:3 * Q], b_stack[2 * Q:3 * Q].bitcast(F32),
                                        ALU.subtract).then_inc(b_lo_ok, 1)

            def h_rest(b):
                dve.wait_ge(h_hi_ok, b + 1)
                nc.vector.tensor_tensor(h_stack[Q:2 * Q], ps_h[Q:2 * Q], h_stack[Q:2 * Q].bitcast(F32),
                                        ALU.subtract).then_inc(h_lo_ok, 1)

            def x2_out(b):
                before(dve, x_ok[3], b)
                dve.wait_ge(mm[1], b + 1)
                nc.vector.tensor_tensor(x_n[2][:], ps_31[:], x_n[1][:], ALU.add).then_inc(x_ok[2], 1)

            def x3_out(b):
                dve.wait_ge(mm[2], b + 1)
                nc.vector.tensor_tensor(x_n[3][:], ps_20[:], x_n[2][:], ALU.add).then_inc(x_ok[3], 1)

            def y_out(b):
                dve.wait_ge(diff_ok, b + 1)
                dve.wait_ge(mm[3], b + 1)
                before(dve, y_st, 16 * b)
                nc.vector.tensor_tensor(y_n[:], ps_31[:], diff[:], ALU.add).then_inc(y_ok, 1)

            def step(t):
                w2_turn(t - 1)
                x_rest(1, t - 1)
                b_turn(t)
                y_out(t - 3)
                x3_out(t - 2)
                x_rest(0, t)
                a_rest(t)
                w1_turn(t)
                x2_out(t - 1)
                x_rest(3, t - 2)
                b_rest(t)
                h_rest(t)
                w2_rest(t - 1)
                x_rest(2, t - 1)

            x_rest(0, 0)
            units_rest(base_lo, base_hi, BASE)
            dve.wait_ge(bias_hi_ok, 1)
            nc.vector.tensor_tensor(bias_lo[:], bias_rows[:], bias_hi[:].bitcast(F32), ALU.subtract).then_inc(bias_lo_ok, 1)
            a_rest(0)
            b_turn(0)
            b_rest(0)
            h_rest(0)
            x_rest(0, 1)
            units_rest(w1_lo, w1_hi, W1, range(0, C // 2))
            b_turn(1)
            a_rest(1)
            units_rest(w1_lo, w1_hi, W1, range(C // 2, C))
            b_rest(1)
            x_rest(1, 0)
            h_rest(1)
            units_rest(w2_lo, w2_hi, W2, range(0, C // 2))
            x_rest(0, 2)
            units_rest(w2_lo, w2_hi, W2, range(C // 2, C - 1))
            b_turn(2)
            a_rest(2)
            units_rest(w2_lo, w2_hi, W2, range(C - 1, C))
            x2_out(0)
            b_rest(2)
            w1_turn(1, range(0, C // 2))
            h_rest(2)
            x_rest(2, 0)
            w1_turn(1, range(C // 2, C))
            x_rest(1, 1)
            w_rest(w1_lo, w1_t, w1_hi, 1, w1_hi_ok, w1_lo_ok, [1])
            x3_out(0)
            w2_turn(1)
            units_rest(w3_lo, w3_hi, W3, range(0, 2))
            x_rest(3, 0)
            x2_out(1)
            units_rest(w3_lo, w3_hi, W3, range(2, C))
            w2_rest(1)
            x_rest(2, 1)
            w1_turn(2)
            step(3)
            with dve.Fori(*LOOP) as t:
                step(t)
            w2_turn(NB - 1)
            x_rest(1, NB - 1)
            y_out(NB - 3)
            x3_out(NB - 2)
            x_rest(3, NB - 2)
            x2_out(NB - 1)
            w2_rest(NB - 1)
            x_rest(2, NB - 1)
            x3_out(NB - 1)
            y_out(NB - 2)
            x_rest(3, NB - 1)
            y_out(NB - 1)

        @block.tensor
        def _(pe):
            def units_turn(raw, n, ready, units=range(C)):
                for k in units:
                    pe.wait_ge(*ready(k))
                    before(pe, unit_lo, unit_after(n + k))
                    bank = unit_bank(n + k)
                    for c in range(C):
                        last = nc.tensor.transpose(bank[:, c, :], raw[:, k, c:D:C], ident[:])
                    last.then_inc(unit_tp, 1)

            def x_turn(l, b):
                if l > 0:
                    pe.wait_ge(x_ok[l], b + 1)
                elif not isinstance(b, int) or b > 1:
                    pe.wait_ge(x_ld, 16 * b)
                else:
                    pe.wait_ge((x_ld, x_spare_ld)[b], 16)
                rows = spare(0, b) if l == 0 else l
                if l == 0 and isinstance(b, int) and b == 1:
                    pe.wait_ge(x_lo_ok[0], 1)
                for c in range(C):
                    last = nc.tensor.transpose(ps_xt[1 - l % 2][:, c, :], x_n[rows][:, c:D:C], ident[:])
                last.then_inc(x_tp[l], 1)

            def a_turn(b):
                if isinstance(b, int):
                    pe.wait_ge(a_ld, 16 * (b + 1))
                for c in range(C):
                    last = nc.tensor.transpose(ps_at[:, c, :], a_raw[:, c:D:C], ident[0:R, 0:R])
                last.then_inc(a_tp, 1)

            def products(dst, x, hi, lo, chunks=range(C), closes=True):
                for c in chunks:
                    nc.tensor.matmul(dst, x_hi[x][:, c], hi[:, c], start=(c == 0), stop=False)
                    nc.tensor.matmul(dst, x_hi[x][:, c], lo[:, c], start=False, stop=False)
                    last = nc.tensor.matmul(dst, x_lo[x][:, c], hi[:, c], start=False, stop=(closes and c == C - 1))
                return last

            def first_layer0():
                pe.wait_ge(unit_hi, BASE + C)
                pe.wait_ge(x_lo_ok[0], 1)
                for c in range(C):
                    nc.tensor.matmul(ps_20[:], x_hi[0][:, c], base_hi[:, c], start=(c == 0), stop=False)
                    nc.tensor.matmul(ps_20[:], x_lo[0][:, c], base_hi[:, c], start=False, stop=False)
                h_products(0)
                x_turn(0, 1)
                pe.wait_ge(unit_lo, BASE + C)
                for c in range(C):
                    nc.tensor.matmul(ps_20[:], x_hi[0][:, c], base_lo[:, c], start=False, stop=False)
                pe.wait_ge(bias_put[0], 2 * 16)
                lora_bias(0)

            def h_products(b):
                pe.wait_ge(a_lo_ok, b + 1)
                for c in range(C):
                    a = lora_at[:, c].rearrange("p n r -> p (n r)")
                    nc.tensor.matmul(ps_h, a, x_hi[spare(0, b)][:, c], start=(c == 0), stop=False)
                    last = nc.tensor.matmul(ps_h, a, x_lo[spare(0, b)][:, c], start=False, stop=(c == C - 1))
                last.then_inc(h_mm, 1)

            def layer0(b, between=None):
                pe.wait_ge(x_lo_ok[0], b + 1)
                products(layer0_bank(b), spare(0, b), base_hi, base_lo, range(0, C // 2), closes=False)
                h_products(b)
                if between:
                    between()
                products(layer0_bank(b), spare(0, b), base_hi, base_lo, range(C // 2, C), closes=False)
                lora_bias(b)

            def lora_bias(b):
                pe.wait_ge(h_lo_ok, b + 1)
                pe.wait_ge(b_lo_ok, b + 1)
                nc.tensor.matmul(layer0_bank(b), h_stack[0:3 * Q + 2], b_stack[0:3 * Q + 2],
                                 start=False, stop=True).then_inc(mm[0], 1)

            def layer1(b, between=None):
                pe.wait_ge(x_lo_ok[1], b + 1)
                if isinstance(b, int) and b == 0:
                    pe.wait_ge(unit_lo, W1 + C)
                else:
                    pe.wait_ge(w1_lo_ok, 2 * b)
                before(pe, y_ok, b - 1)
                products(ps_31[:], 1, w1_hi, w1_lo, range(0, C // 2))
                if between:
                    between()
                products(ps_31[:], 1, w1_hi, w1_lo, range(C // 2, C)).then_inc(mm[1], 1)

            def layer2(b):
                pe.wait_ge(x_lo_ok[2], b + 1)
                if isinstance(b, int) and b == 0:
                    pe.wait_ge(unit_lo, W2 + C)
                else:
                    pe.wait_ge(w2_lo_ok, 2 * b)
                products(ps_20[:], 2, w2_hi, w2_lo).then_inc(mm[2], 1)

            def layer3_signs(b):
                pe.wait_ge(x_lo_ok[3], b + 1)
                pe.wait_ge(sign_ok, b + 1)
                before(pe, diff_ok, b)
                for c in range(C):
                    nc.tensor.matmul(ps_sign[:], x_hi[spare(3, b)][:, c], sign[:, c], start=(c == 0), stop=False)
                    last = nc.tensor.matmul(ps_sign[:], x_lo[spare(3, b)][:, c], sign[:, c], start=False, stop=(c == C - 1))
                last.then_inc(mm_sign, 1)

            def layer3(b, chunks=range(C)):
                last = products(ps_31[:], spare(3, b), w3_hi, w3_lo, chunks, closes=False)
                if C - 1 in chunks:
                    nc.tensor.matmul(ps_31[:], ones2[:], bias3[:], start=False, stop=True).then_inc(mm[3], 1)

            def step(t):
                layer3_signs(t - 3)
                layer3(t - 3)
                x_turn(1, t - 1)
                layer2(t - 2)
                pe.wait_ge(a_ld, 16 * (t + 1))
                x_turn(0, t)
                a_turn(t)
                layer1(t - 1, lambda: x_turn(3, t - 2))
                layer0(t)
                x_turn(2, t - 1)

            pe.wait_ge(ident_ok, 1)
            for k in range(WARM_UP):
                nc.tensor.transpose(ps_31[:, 0:P], ident[:], ident[:])
            x_turn(0, 0)
            units_turn(base_raw, BASE, lambda k: (base_diag_ok, k + 1))
            a_turn(0)
            pe.wait_ge(ones_ok, 2)
            first_layer0()
            units_turn(as_loaded(w1_raw), W1, lambda k: (first_ld[0][k], 16))
            a_turn(1)
            x_turn(1, 0)
            layer0(1)
            units_turn(as_loaded(w2_raw), W2, lambda k: (first_ld[1][k], 16), range(0, C // 2))
            x_turn(0, 2)
            units_turn(as_loaded(w2_raw), W2, lambda k: (first_ld[1][k], 16), range(C // 2, C - 1))
            layer1(0)
            a_turn(2)
            units_turn(as_loaded(w2_raw), W2, lambda k: (first_ld[1][k], 16), range(C - 1, C))
            layer0(2, lambda: x_turn(2, 0))
            x_turn(1, 1)
            layer2(0)
            units_turn(w3_raw, W3, lambda k: (w3_diag_ok, k + 1), range(0, 2))
            layer1(1, lambda: x_turn(3, 0))
            units_turn(w3_raw, W3, lambda k: (w3_diag_ok, k + 1), range(2, C))
            x_turn(2, 1)
            pe.wait_ge(unit_lo, W3 + C)
            pe.wait_ge(bias_put[1], 2 * 16)
            step(3)
            with pe.Fori(*LOOP) as t:
                step(t)
            layer3_signs(NB - 3)
            layer3(NB - 3)
            x_turn(1, NB - 1)
            layer2(NB - 2)
            layer1(NB - 1, lambda: x_turn(3, NB - 2))
            layer3_signs(NB - 2)
            x_turn(2, NB - 1)
            layer3(NB - 2, range(C // 2))
            layer2(NB - 1)
            layer3(NB - 2, range(C // 2, C - 1))
            x_turn(3, NB - 1)
            layer3(NB - 2, range(C - 1, C))
            layer3_signs(NB - 1)
            layer3(NB - 1)


_INS = ['x', 'itok_B_6_15', 'itok_B_3_7', 'itok_B_1_14', 'condB_coeff', 'mask_Bx4096x4096_ik1',
        'L0_cond_base_weight', 'L0_cond_base_bias', 'L0_cond_lora_A_w', 'L0_cond_lora_B_w',
        'L1_cond_weight', 'L2_cond_weight', 'L3_cond_W', 'L3_cond_b']


def kernel(**inputs):
    import numpy as _np
    import concourse.bacc as _bacc
    from concourse import mybir as _mybir
    from concourse.bass_utils import run_bass_kernel_spmd as _run

    nc = _bacc.Bacc("TRN2", target_bir_lowering=False, num_devices=1)
    arrays, args = {}, []
    for name in _INS:
        a = _np.ascontiguousarray(inputs[name])
        arrays[f"in_{name}_dram"] = a
        args.append(nc.dram_tensor(f"in_{name}_dram", a.shape, _mybir.dt.from_np(a.dtype), kind="ExternalInput").ap())
    shape = inputs['x'].shape
    args.append(nc.dram_tensor("out_0_dram", shape, _mybir.dt.from_np(_np.dtype('float32')), kind="ExternalOutput").ap())
    adapter_chain(nc, *args)
    r = _run(nc, [arrays], core_ids=[0])
    return r.results[0]["out_0_dram"]
```

```python
from contextlib import ExitStack

import concourse.bass as bass
from concourse import mybir

ALU = mybir.AluOpType
ACT = mybir.ActivationFunctionType
F32 = mybir.dt.float32
F32R = mybir.dt.float32r
I32 = mybir.dt.int32

P = 128
Q = 32


def adapter_chain(nc, x, ids_lora, ids_w1, ids_w2, coeff, mask, base_w, base_b, lora_a, lora_b, w1, w2, w3, b3, out):
    NB, S, D = x.shape
    C = D // P
    R = lora_a.shape[1]
    KB = D // Q
    assert S == P and D == P * C and 2 * R == Q and R * C <= P

    ctx = ExitStack()
    with ctx:
        def sb(name, shape, dt=F32):
            return ctx.enter_context(nc.sbuf_tensor(name, shape, dt))

        def ps(name, shape):
            return ctx.enter_context(nc.psum_tensor(name, shape, F32))

        def sem(name):
            return ctx.enter_context(nc.semaphore(name))

        ident = sb("ident", [P, P])
        ids = sb("ids", [1, 3 * NB], I32)
        coeff_all = sb("coeff_all", [P, NB])
        bias0 = sb("bias0", [1, D])
        bias0_hi = sb("bias0_hi", [1, D], F32R)
        bias0_lo = sb("bias0_lo", [1, D], F32R)
        bias3 = sb("bias3", [P, D])
        base_raw = sb("base_raw", [P, C, D])
        w3_raw = sb("w3_raw", [P, C, D])
        base_hi = sb("base_hi", [P, C, D], F32R)
        base_lo = sb("base_lo", [P, C, D], F32R)
        w3_hi = sb("w3_hi", [P, C, D], F32R)
        w3_lo = sb("w3_lo", [P, C, D], F32R)
        w1_raw = sb("w1_raw", [P, KB, P])
        w2_raw = sb("w2_raw", [P, KB, P])
        w1_t = sb("w1_t", [P, C, D])
        w2_t = sb("w2_t", [P, C, D])
        w1_hi = sb("w1_hi", [P, C, D], F32R)
        w1_lo = sb("w1_lo", [P, C, D], F32R)
        w2_hi = sb("w2_hi", [P, C, D], F32R)
        w2_lo = sb("w2_lo", [P, C, D], F32R)
        mask_raw = sb("mask_raw", [P, C * D], I32)
        sign = sb("sign", [P, C, D], F32R)
        a_raw = sb("a_raw", [R, D])
        lora_at = sb("lora_at", [P, C, 3, 2 * R], F32R)
        b_raw = sb("b_raw", [3 * Q, KB, R])
        b_t = sb("b_t", [3 * Q, D])
        h_stack = sb("h_stack", [P, S], F32R)
        b_stack = sb("b_stack", [P, D], F32R)
        x_n = [sb(f"x{l}_n", [P, D]) for l in range(4)]
        x_hi = [sb(f"x{l}_hi", [P, C, S], F32R) for l in range(4)]
        x_lo = [sb(f"x{l}_lo", [P, C, S], F32R) for l in range(4)]
        diff = sb("diff", [P, D])
        y_n = sb("y_n", [P, D])

        ps_31 = ps("ps_31", [P, D])
        ps_sign = ps("ps_sign", [P, D])
        ps_20 = ps("ps_20", [P, D])
        ps_xt = [ps(f"ps_xt{k}", [P, C, S]) for k in range(2)]
        ps_lora = ps("ps_lora", [P, 512])
        ps_wt = [ps(f"ps_wt{k}", [P, C, P]) for k in range(2)]
        ps_h = ps_lora[0:3 * 2 * R, 0:S]
        ps_at = ps_lora[:, S:S + C * R].rearrange("p (c r) -> p c r", c=C)

        ids_ld = [sem(f"ids{k}_ld") for k in range(3)]
        coeff_ld = sem("coeff_ld")
        bias0_ld = sem("bias0_ld")
        bias0_put = sem("bias0_put")
        bias3_ld = sem("bias3_ld")
        base_ld = [sem(f"base_ld{k}") for k in range(C)]
        w3_ld = [sem(f"w3_ld{k}") for k in range(C)]
        w1_first_ld = [sem(f"w1_first_ld{k}") for k in range(C)]
        w2_first_ld = [sem(f"w2_first_ld{k}") for k in range(C)]
        x_ld = sem("x_ld")
        x_spare_ld = sem("x_spare_ld")
        a_ld = sem("a_ld")
        b_ld = sem("b_ld")
        w1_ld = sem("w1_ld")
        w2_ld = sem("w2_ld")
        mask_ld = sem("mask_ld")
        y_st = sem("y_st")
        ident_zero = sem("ident_zero")
        ident_ok = sem("ident_ok")
        ones_ok = sem("ones_ok")
        bias_hi_ok = sem("bias_hi_ok")
        bias_lo_ok = sem("bias_lo_ok")
        base_diag_ok = sem("base_diag_ok")
        w3_diag_ok = sem("w3_diag_ok")
        unit_tp = sem("unit_tp")
        unit_hi = sem("unit_hi")
        unit_lo = sem("unit_lo")
        x_tp = [sem(f"x{l}_tp") for l in range(4)]
        x_hi_ok = [sem(f"x{l}_hi_ok") for l in range(4)]
        x_lo_ok = [sem(f"x{l}_lo_ok") for l in range(4)]
        x_ok = [None] + [sem(f"x{l}_ok") for l in range(1, 4)]
        mm = [sem(f"mm{l}") for l in range(4)]
        mm_sign = sem("mm_sign")
        a_tp = sem("a_tp")
        a_hi_ok = sem("a_hi_ok")
        a_lo_ok = sem("a_lo_ok")
        h_mm = sem("h_mm")
        h_hi_ok = sem("h_hi_ok")
        h_lo_ok = sem("h_lo_ok")
        b_tp = sem("b_tp")
        b_hi_ok = sem("b_hi_ok")
        b_lo_ok = sem("b_lo_ok")
        w1_tp = sem("w1_tp")
        w2_tp = sem("w2_tp")
        w1_hi_ok = sem("w1_hi_ok")
        w2_hi_ok = sem("w2_hi_ok")
        w1_lo_ok = sem("w1_lo_ok")
        w2_lo_ok = sem("w2_lo_ok")
        sign_ok = sem("sign_ok")
        diff_ok = sem("diff_ok")
        diff_bias_ok = sem("diff_bias_ok")
        y_ok = sem("y_ok")
        y_bias_ok = sem("y_bias_ok")

        LOOP = (4, NB)
        BASE, W1, W2, W3 = range(0, 4 * C, C)
        WARM_UP = 12

        def before(eng, s, n):
            if not isinstance(n, int) or n > 0:
                eng.wait_ge(s, n)

        def spare(l, b):
            return 3 - l if isinstance(b, int) and (l, b) in ((0, 1), (3, NB - 1)) else l

        halves = [(h * C // 2, (h + 1) * C // 2) for h in range(2)]
        cols = [(h * D // 2, (h + 1) * D // 2) for h in range(2)]
        ps_last = [ps_20, ps_31]

        def unit_bank(n):
            banks = [ps_wt[0], ps_wt[1], ps_sign, ps_31]
            if n >= W3:
                banks = [ps_wt[0], ps_sign, ps_wt[0], ps_20]
            elif n >= W2:
                banks = [ps_wt[0], ps_wt[1], ps_sign, ps_wt[0]]
            bank = banks[n % C]
            return bank[:] if bank in ps_wt else bank[:].rearrange("p (c o) -> p c o", c=C)

        def unit_after(n):
            return n - C + 1 if n < W2 else (max(W2, n - 2) if n < W3 else max(W3, n - 1))

        def layer0_bank(b):
            return ps_wt[1][:].rearrange("p c o -> p (c o)") if isinstance(b, int) and b == 2 else ps_20[:]

        def as_loaded(raw):
            return raw[:].rearrange("p k j -> p (k j)").rearrange("p (n i) -> p n i", i=D)

        block = ctx.enter_context(nc.Block())

        @block.sync
        def _(sp):
            def index(k, b, count):
                return sp.value_load(ids[0:1, bass.ds(b + k * NB, 1)], min_val=0, max_val=count - 1)

            def load_x(b):
                before(sp, x_tp[0], b)
                sp.dma_start(x_n[0][:], x[bass.ds(b, 1)].rearrange("a s d -> (a s) d")).then_inc(x_ld, 16)

            def load_lora(b):
                i = index(0, b, lora_a.shape[0])
                before(sp, a_tp, b)
                sp.dma_start(a_raw[:], lora_a[bass.ds(i, 1)].rearrange("a r d -> (a r) d")).then_inc(a_ld, 16)
                before(sp, b_tp, b)
                for q in range(3):
                    sp.dma_start(b_raw[q * Q:(q + 1) * Q],
                                 lora_b[bass.ds(i, 1)].rearrange("a (p k) r -> (a p) k r", k=KB)).then_inc(b_ld, 16)

            def load_rows(dst, src, k, s):
                sp.dma_start(dst[:, k, :], src[k * P:(k + 1) * P, :]).then_inc(s[k], 16)

            def load_first(dst, weights, n, s, units=range(C)):
                i = index(n, 0, weights.shape[0])
                for k in units:
                    src = weights[bass.ds(i, 1), k * P:(k + 1) * P, :].rearrange("a p i -> (a p) i")
                    sp.dma_start(as_loaded(dst)[:, k, :], src).then_inc(s[k], 16)

            def load_adapter(dst, weights, k, b, tp, s):
                i = index(k, b, weights.shape[0])
                if isinstance(b, int) and b == 1:
                    sp.wait_ge(unit_tp, (W1, W2)[k - 1] + C)
                else:
                    sp.wait_ge(tp, (b - 1) * C)
                for q in range(P // Q):
                    src = weights[bass.ds(i, 1), :, q * P:(q + 1) * P]
                    sp.dma_start(dst[q * Q:(q + 1) * Q], src.rearrange("a (k r) i -> (a r) k i", r=Q)).then_inc(s, 16)

            def load_mask(b):
                before(sp, sign_ok, b)
                sp.dma_start(mask_raw[:], mask[bass.ds(b, 1)].rearrange("a (p c) o -> (a p) (c o)", c=C)).then_inc(mask_ld, 16)

            def store_y(b):
                sp.wait_ge(y_bias_ok, b + 1)
                sp.dma_start(out[bass.ds(b, 1)].rearrange("a s d -> (a s) d"), y_n[:]).then_inc(y_st, 16)

            def step(t):
                load_x(t)
                load_lora(t)
                load_adapter(w1_raw, w1, 1, t, w1_tp, w1_ld)
                load_adapter(w2_raw, w2, 2, t, w2_tp, w2_ld)
                store_y(t - 3)
                load_mask(t - 1)

            load_x(0)
            for k in range(C):
                load_rows(base_raw, base_w, k, base_ld)
            sp.wait_ge(ids_ld[0], 16)
            load_lora(0)
            sp.dma_start(x_n[spare(0, 1)][:], x[1]).then_inc(x_spare_ld, 16)
            sp.wait_ge(ids_ld[1], 16)
            load_first(w1_raw, w1, 1, w1_first_ld)
            load_lora(1)
            sp.wait_ge(ids_ld[2], 16)
            load_first(w2_raw, w2, 2, w2_first_ld, range(0, C // 2))
            load_x(2)
            load_first(w2_raw, w2, 2, w2_first_ld, range(C // 2, C))
            load_lora(2)
            load_adapter(w1_raw, w1, 1, 1, w1_tp, w1_ld)
            for k in range(C):
                load_rows(w3_raw, w3, k, w3_ld)
            load_adapter(w2_raw, w2, 2, 1, w2_tp, w2_ld)
            load_mask(0)
            load_adapter(w1_raw, w1, 1, 2, w1_tp, w1_ld)
            load_x(3)
            load_lora(3)
            load_mask(1)
            load_adapter(w2_raw, w2, 2, 2, w2_tp, w2_ld)
            load_adapter(w1_raw, w1, 1, 3, w1_tp, w1_ld)
            load_mask(2)
            load_adapter(w2_raw, w2, 2, 3, w2_tp, w2_ld)
            store_y(0)
            with sp.Fori(*LOOP) as t:
                step(t)
            store_y(NB - 3)
            load_mask(NB - 1)
            store_y(NB - 2)
            for h, (a, e) in enumerate(cols):
                sp.wait_ge(y_ok, NB + h)
                sp.dma_start(out[NB - 1, :, a:e], diff[:, a:e]).then_inc(y_st, 16)
            sp.wait_ge(y_st, 16 * (NB + 1))

        @block.gpsimd
        def _(pool):
            nc.gpsimd.memset(ident[:], 0.0).then_inc(ident_zero, 1)
            pool.wait_ge(ident_zero, 1)
            nc.gpsimd.affine_select(out=ident[:], in_=ident[:], compare_op=ALU.not_equal, fill=1.0, base=0,
                                    pattern=[[-1, P]], channel_multiplier=1).then_inc(ident_ok, 1)
            pool.dma_start(bias0[:], base_b.rearrange("(a b) -> a b", a=1)).then_inc(bias0_ld, 16)
            pool.wait_ge(ident_ok, 1)
            nc.gpsimd.memset(h_stack[3 * Q:P].bitcast(F32), 1.0).then_inc(ones_ok, 1)
            pool.wait_ge(ones_ok, 1)
            pool.dma_start(coeff_all[:], coeff.rearrange("(a b) -> a b", a=1).broadcast_to([P, NB])).then_inc(coeff_ld, 16)

            def add_diag(raw, k, ok):
                v = raw[:, k, k * P:(k + 1) * P]
                nc.gpsimd.tensor_tensor(v, v, ident[:], ALU.add).then_inc(ok, 1)
                pool.wait_ge(ok, k + 1)

            def w_rest(lo, t_, hi, b, hi_ok, lo_ok, parts):
                for h in parts:
                    a, e = halves[h]
                    pool.wait_ge(hi_ok, 2 * (b - 1) + h + 1)
                    nc.gpsimd.tensor_tensor(lo[:, a:e], t_[:, a:e], hi[:, a:e].bitcast(F32), ALU.subtract).then_inc(lo_ok, 1)

            def w1_rest(b, parts):
                w_rest(w1_lo, w1_t, w1_hi, b, w1_hi_ok, w1_lo_ok, parts)

            def w2_rest(b, parts):
                w_rest(w2_lo, w2_t, w2_hi, b, w2_hi_ok, w2_lo_ok, parts)

            def add_bias3(b):
                pool.wait_ge(y_ok, b + 1)
                nc.gpsimd.tensor_tensor(y_n[:], y_n[:], bias3[:], ALU.add).then_inc(y_bias_ok, 1)

            def step(t):
                add_bias3(t - 3)
                w1_rest(t, [0, 1])

            for k in range(C):
                pool.wait_ge(base_ld[k], 16)
                add_diag(base_raw, k, base_diag_ok)
            pool.dma_start(bias3[:], b3.rearrange("(a b) -> a b", a=1).broadcast_to([P, D])).then_inc(bias3_ld, 16)
            for k in range(C):
                pool.wait_ge(w3_ld[k], 16)
                add_diag(w3_raw, k, w3_diag_ok)
            w1_rest(1, [0])
            w2_rest(1, [0, 1])
            w1_rest(2, [0, 1])
            pool.wait_ge(bias3_ld, 16)
            add_bias3(0)
            w2_rest(2, [0, 1])
            w1_rest(3, [0, 1])
            with pool.Fori(*LOOP) as t:
                step(t)
            add_bias3(NB - 3)
            w2_rest(NB - 1, [0])
            add_bias3(NB - 2)

        @block.scalar
        def _(act):
            for k, v in enumerate((ids_lora, ids_w1, ids_w2)):
                act.dma_start(ids[:, k * NB:(k + 1) * NB], v.rearrange("(a b) -> a b", a=1)).then_inc(ids_ld[k], 16)

            def units_round(dst, n, units=range(C)):
                for k in units:
                    act.wait_ge(unit_tp, n + k + 1)
                    nc.scalar.activation(dst[:, :, k * P:(k + 1) * P], unit_bank(n + k), ACT.Copy).then_inc(unit_hi, 1)

            def x_round(l, b):
                act.wait_ge(x_tp[l], b + 1)
                if spare(l, b) == l:
                    before(act, mm[l], b)
                nc.scalar.activation(x_hi[spare(l, b)][:], ps_xt[1 - l % 2][:], ACT.Copy).then_inc(x_hi_ok[l], 1)

            def w_round(dst, src, b, tp, used, ok, parts=(0, 1)):
                for h in parts:
                    a, e = halves[h]
                    act.wait_ge(tp, C * (b - 1) + e)
                    if h == 0:
                        act.wait_ge(used, b)
                    nc.scalar.activation(dst[:, a:e], src[:, a:e], ACT.Copy).then_inc(ok, 1)

            def w1_round(b, parts=(0, 1)):
                w_round(w1_hi, w1_t, b, w1_tp, mm[1], w1_hi_ok, parts)

            def w2_round(b, parts=(0, 1)):
                w_round(w2_hi, w2_t, b, w2_tp, mm[2], w2_hi_ok, parts)

            def a_round(b):
                act.wait_ge(a_tp, b + 1)
                before(act, h_mm, b)
                nc.scalar.activation(lora_at[:, :, :, 0:R], ps_at.unsqueeze(2).broadcast_to([P, C, 3, R]),
                                     ACT.Copy).then_inc(a_hi_ok, 1)

            def b_round(b):
                act.wait_ge(b_tp, b + 1)
                before(act, mm[0], b)
                nc.scalar.activation(b_stack[0:3 * Q], b_t[:], ACT.Copy).then_inc(b_hi_ok, 1)

            def h_round(b):
                act.wait_ge(h_mm, b + 1)
                nc.scalar.activation(h_stack[0:3 * Q], ps_h, ACT.Copy).then_inc(h_hi_ok, 1)

            def x1_out(b):
                act.wait_ge(mm[0], b + 1)
                before(act, x_ok[2], b)
                nc.scalar.activation(x_n[1][:], layer0_bank(b), ACT.Copy).then_inc(x_ok[1], 1)

            def signs(b):
                act.wait_ge(mask_ld, 16 * (b + 1))
                before(act, mm_sign, b)
                nc.scalar.activation(sign[:].rearrange("p c o -> p (c o)"), mask_raw[:], ACT.Copy,
                                     scale=2.0, bias=-1.0).then_inc(sign_ok, 1)

            def scale_diff(b):
                act.wait_ge(mm_sign, b + 1)
                before(act, y_ok, b)
                nc.scalar.activation(diff[:], ps_sign[:], ACT.Copy,
                                     scale=coeff_all[:, bass.ds(b, 1)]).then_inc(diff_ok, 1)

            def step(t):
                x_round(1, t - 1)
                scale_diff(t - 3)
                signs(t - 2)
                x_round(0, t)
                a_round(t)
                w2_round(t - 1)
                x_round(3, t - 2)
                b_round(t)
                h_round(t)
                w1_round(t)
                x1_out(t)
                x_round(2, t - 1)

            x_round(0, 0)
            act.wait_ge(bias0_ld, 16)
            nc.scalar.activation(bias0_hi[:], bias0[:], ACT.Copy).then_inc(bias_hi_ok, 1)
            units_round(base_hi, BASE)
            a_round(0)
            act.wait_ge(bias_lo_ok, 1)
            for n, part in enumerate((bias0_hi, bias0_lo)):
                row = b_stack[3 * Q + n:3 * Q + n + 1]
                act.dma_start(row.bitcast(F32), part[:].bitcast(F32)).then_inc(bias0_put, 16)
            b_round(0)
            h_round(0)
            x_round(0, 1)
            x1_out(0)
            units_round(w1_hi, W1)
            a_round(1)
            x_round(1, 0)
            b_round(1)
            h_round(1)
            units_round(w2_hi, W2, range(0, C // 2))
            x_round(0, 2)
            units_round(w2_hi, W2, range(C // 2, C - 1))
            a_round(2)
            units_round(w2_hi, W2, range(C - 1, C))
            b_round(2)
            x1_out(1)
            h_round(2)
            x_round(2, 0)
            w1_round(1, [0])
            x_round(1, 1)
            w1_round(1, [1])
            units_round(w3_hi, W3, range(0, C // 2))
            signs(0)
            x_round(3, 0)
            w2_round(1, [0])
            units_round(w3_hi, W3, range(C // 2, C))
            w2_round(1, [1])
            x1_out(2)
            x_round(2, 1)
            w1_round(2)
            act.wait_ge(coeff_ld, 16)
            x_round(1, 2)
            scale_diff(0)
            signs(1)
            x_round(0, 3)
            a_round(3)
            b_round(3)
            x_round(3, 1)
            w2_round(2, [0])
            h_round(3)
            w2_round(2, [1])
            x1_out(3)
            x_round(2, 2)
            w1_round(3)
            with act.Fori(*LOOP) as t:
                step(t)
            x_round(1, NB - 1)
            scale_diff(NB - 3)
            signs(NB - 2)
            w2_round(NB - 1, [0])
            x_round(3, NB - 2)
            w2_round(NB - 1, [1])
            x_round(2, NB - 1)
            scale_diff(NB - 2)
            signs(NB - 1)
            x_round(3, NB - 1)
            scale_diff(NB - 1)

        @block.vector
        def _(dve):
            def units_rest(lo, hi, n, units=range(C)):
                for k in units:
                    dve.wait_ge(unit_hi, n + k + 1)
                    nc.vector.tensor_tensor(lo[:, :, k * P:(k + 1) * P], unit_bank(n + k),
                                            hi[:, :, k * P:(k + 1) * P].bitcast(F32), ALU.subtract).then_inc(unit_lo, 1)

            def x_rest(l, b):
                dve.wait_ge(x_hi_ok[l], b + 1)
                nc.vector.tensor_tensor(x_lo[spare(l, b)][:], ps_xt[1 - l % 2][:], x_hi[spare(l, b)][:].bitcast(F32),
                                        ALU.subtract).then_inc(x_lo_ok[l], 1)

            def w_turn(dst, raw, b, ld, used, tp, chunks=range(C)):
                dve.wait_ge(ld, 16 * (P // Q) * b)
                before(dve, used, 2 * (b - 1))
                for c in chunks:
                    nc.vector.transpose(dst[:, c, :].rearrange("p (k j) -> p k j", j=Q),
                                        raw[:].rearrange("p k (j c) -> p c k j", c=C)[:, c]).then_inc(tp, 1)

            def w1_turn(b, chunks=range(C)):
                w_turn(w1_t, w1_raw, b, w1_ld, w1_lo_ok, w1_tp, chunks)

            def w2_turn(b, chunks=range(C)):
                w_turn(w2_t, w2_raw, b, w2_ld, w2_lo_ok, w2_tp, chunks)

            def w_rest(lo, t_, hi, b, hi_ok, lo_ok, parts):
                for h in parts:
                    a, e = halves[h]
                    dve.wait_ge(hi_ok, 2 * (b - 1) + h + 1)
                    nc.vector.tensor_tensor(lo[:, a:e], t_[:, a:e], hi[:, a:e].bitcast(F32), ALU.subtract).then_inc(lo_ok, 1)

            def w2_rest(b):
                w_rest(w2_lo, w2_t, w2_hi, b, w2_hi_ok, w2_lo_ok, [0, 1])

            def a_rest(b):
                dve.wait_ge(a_hi_ok, b + 1)
                nc.vector.tensor_tensor(lora_at[:, :, :, R:2 * R], ps_at.unsqueeze(2).broadcast_to([P, C, 3, R]),
                                        lora_at[:, :, :, 0:R].bitcast(F32), ALU.subtract).then_inc(a_lo_ok, 1)

            def b_turn(b):
                dve.wait_ge(b_ld, 3 * 16 * (b + 1))
                before(dve, b_lo_ok, b)
                nc.vector.transpose(b_t[:].rearrange("q (p k) -> q k p", k=KB),
                                    b_raw[:].unsqueeze(2).broadcast_to([3 * Q, KB, 2, R])).then_inc(b_tp, 1)

            def b_rest(b):
                dve.wait_ge(b_hi_ok, b + 1)
                nc.vector.tensor_tensor(b_stack[2 * Q:3 * Q], b_t[2 * Q:3 * Q], b_stack[2 * Q:3 * Q].bitcast(F32),
                                        ALU.subtract).then_inc(b_lo_ok, 1)

            def h_rest(b):
                dve.wait_ge(h_hi_ok, b + 1)
                nc.vector.tensor_tensor(h_stack[Q:2 * Q], ps_h[Q:2 * Q], h_stack[Q:2 * Q].bitcast(F32),
                                        ALU.subtract).then_inc(h_lo_ok, 1)

            def x2_out(b):
                before(dve, x_ok[3], b)
                dve.wait_ge(mm[1], b + 1)
                nc.vector.tensor_tensor(x_n[2][:], ps_31[:], x_n[1][:], ALU.add).then_inc(x_ok[2], 1)

            def x3_out(b):
                dve.wait_ge(mm[2], b + 1)
                nc.vector.tensor_tensor(x_n[3][:], ps_20[:], x_n[2][:], ALU.add).then_inc(x_ok[3], 1)

            def y_out(b):
                dve.wait_ge(diff_ok, b + 1)
                dve.wait_ge(mm[3], b + 1)
                before(dve, y_st, 16 * b)
                nc.vector.tensor_tensor(y_n[:], ps_31[:], diff[:], ALU.add).then_inc(y_ok, 1)

            def step(t):
                w2_turn(t - 1)
                x_rest(1, t - 1)
                y_out(t - 3)
                b_turn(t)
                x3_out(t - 2)
                x_rest(0, t)
                a_rest(t)
                w1_turn(t)
                x2_out(t - 1)
                x_rest(3, t - 2)
                b_rest(t)
                h_rest(t)
                w2_rest(t - 1)
                x_rest(2, t - 1)

            x_rest(0, 0)
            dve.wait_ge(bias_hi_ok, 1)
            nc.vector.tensor_tensor(bias0_lo[:], bias0[:], bias0_hi[:].bitcast(F32), ALU.subtract).then_inc(bias_lo_ok, 1)
            units_rest(base_lo, base_hi, BASE)
            a_rest(0)
            b_turn(0)
            b_rest(0)
            h_rest(0)
            x_rest(0, 1)
            units_rest(w1_lo, w1_hi, W1, range(0, C - 1))
            a_rest(1)
            b_turn(1)
            units_rest(w1_lo, w1_hi, W1, range(C - 1, C))
            b_rest(1)
            h_rest(1)
            x_rest(1, 0)
            units_rest(w2_lo, w2_hi, W2, range(0, C // 2))
            x_rest(0, 2)
            units_rest(w2_lo, w2_hi, W2, range(C // 2, C - 1))
            b_turn(2)
            a_rest(2)
            units_rest(w2_lo, w2_hi, W2, range(C - 1, C))
            x2_out(0)
            b_rest(2)
            w1_turn(1, range(0, C // 2))
            h_rest(2)
            x_rest(2, 0)
            w1_turn(1, range(C // 2, C))
            x_rest(1, 1)
            w_rest(w1_lo, w1_t, w1_hi, 1, w1_hi_ok, w1_lo_ok, [1])
            x3_out(0)
            units_rest(w3_lo, w3_hi, W3, range(0, C // 2))
            w2_turn(1, range(0, C // 2))
            x2_out(1)
            x_rest(3, 0)
            w2_turn(1, range(C // 2, C))
            units_rest(w3_lo, w3_hi, W3, range(C // 2, C))
            w1_turn(2)
            x_rest(2, 1)
            x_rest(1, 2)
            y_out(0)
            b_turn(3)
            x3_out(1)
            x_rest(0, 3)
            a_rest(3)
            b_rest(3)
            w2_turn(2)
            h_rest(3)
            x2_out(2)
            x_rest(3, 1)
            w1_turn(3)
            x_rest(2, 2)
            with dve.Fori(*LOOP) as t:
                step(t)
            w2_turn(NB - 1)
            x_rest(1, NB - 1)
            y_out(NB - 3)
            x3_out(NB - 2)
            x_rest(3, NB - 2)
            x2_out(NB - 1)
            w_rest(w2_lo, w2_t, w2_hi, NB - 1, w2_hi_ok, w2_lo_ok, [1])
            x_rest(2, NB - 1)
            x3_out(NB - 1)
            x_rest(3, NB - 1)
            y_out(NB - 2)
            dve.wait_ge(bias3_ld, 16)
            dve.wait_ge(diff_ok, NB)
            nc.vector.tensor_tensor(diff[:], diff[:], bias3[:], ALU.add).then_inc(diff_bias_ok, 1)
            dve.wait_ge(diff_bias_ok, 1)
            for h, (a, e) in enumerate(cols):
                dve.wait_ge(mm[3], NB + h)
                nc.vector.tensor_tensor(diff[:, a:e], ps_last[h][:, a:e], diff[:, a:e], ALU.add).then_inc(y_ok, 1)

        @block.tensor
        def _(pe):
            def units_turn(raw, n, ready, units=range(C)):
                for k in units:
                    pe.wait_ge(*ready(k))
                    before(pe, unit_lo, unit_after(n + k))
                    bank = unit_bank(n + k)
                    for c in range(C):
                        last = nc.tensor.transpose(bank[:, c, :], raw[:, k, c:D:C], ident[:])
                    last.then_inc(unit_tp, 1)

            def x_turn(l, b):
                if l > 0:
                    pe.wait_ge(x_ok[l], b + 1)
                elif not isinstance(b, int) or b > 1:
                    pe.wait_ge(x_ld, 16 * b)
                else:
                    pe.wait_ge((x_ld, x_spare_ld)[b], 16)
                rows = spare(0, b) if l == 0 else l
                if l == 0 and isinstance(b, int) and b == 1:
                    pe.wait_ge(x_lo_ok[0], 1)
                for c in range(C):
                    last = nc.tensor.transpose(ps_xt[1 - l % 2][:, c, :], x_n[rows][:, c:D:C], ident[:])
                last.then_inc(x_tp[l], 1)

            def a_turn(b):
                if isinstance(b, int):
                    pe.wait_ge(a_ld, 16 * (b + 1))
                for c in range(C):
                    last = nc.tensor.transpose(ps_at[:, c, :], a_raw[:, c:D:C], ident[0:R, 0:R])
                last.then_inc(a_tp, 1)

            def products(dst, x, hi, lo, chunks=range(C), closes=True):
                for c in chunks:
                    nc.tensor.matmul(dst, x_hi[x][:, c], hi[:, c], start=(c == 0), stop=False)
                    nc.tensor.matmul(dst, x_hi[x][:, c], lo[:, c], start=False, stop=False)
                    last = nc.tensor.matmul(dst, x_lo[x][:, c], hi[:, c], start=False, stop=(closes and c == C - 1))
                return last

            def sweep(dst, a, w, opens=False, closes=False):
                for c in range(C):
                    last = nc.tensor.matmul(dst, a[:, c], w[:, c], start=(opens and c == 0), stop=(closes and c == C - 1))
                return last

            def first_layer0():
                pe.wait_ge(unit_hi, BASE + C)
                pe.wait_ge(x_lo_ok[0], 1)
                sweep(ps_20[:], x_hi[0], base_hi, opens=True)
                sweep(ps_20[:], x_lo[0], base_hi)
                h_products(0)
                x_turn(0, 1)
                pe.wait_ge(unit_lo, BASE + C)
                sweep(ps_20[:], x_hi[0], base_lo)
                pe.wait_ge(bias0_put, 2 * 16)
                lora_bias(0)

            def h_products(b):
                pe.wait_ge(a_lo_ok, b + 1)
                for c in range(C):
                    a = lora_at[:, c].rearrange("p n r -> p (n r)")
                    nc.tensor.matmul(ps_h, a, x_hi[spare(0, b)][:, c], start=(c == 0), stop=False)
                    last = nc.tensor.matmul(ps_h, a, x_lo[spare(0, b)][:, c], start=False, stop=(c == C - 1))
                last.then_inc(h_mm, 1)

            def layer0(b, between=None):
                pe.wait_ge(x_lo_ok[0], b + 1)
                products(layer0_bank(b), spare(0, b), base_hi, base_lo, range(0, C // 2), closes=False)
                h_products(b)
                if between:
                    between()
                products(layer0_bank(b), spare(0, b), base_hi, base_lo, range(C // 2, C), closes=False)
                lora_bias(b)

            def lora_bias(b):
                pe.wait_ge(h_lo_ok, b + 1)
                pe.wait_ge(b_lo_ok, b + 1)
                nc.tensor.matmul(layer0_bank(b), h_stack[0:3 * Q + 2], b_stack[0:3 * Q + 2],
                                 start=False, stop=True).then_inc(mm[0], 1)

            def layer1(b, between=None):
                pe.wait_ge(x_lo_ok[1], b + 1)
                if isinstance(b, int) and b == 0:
                    pe.wait_ge(unit_lo, W1 + C)
                else:
                    pe.wait_ge(w1_lo_ok, 2 * b if isinstance(b, int) and b == 1 else 2 * b - 1)
                before(pe, y_ok, b - 1)
                products(ps_31[:], 1, w1_hi, w1_lo, range(0, C // 2))
                if between:
                    between()
                if not isinstance(b, int) or b > 0:
                    pe.wait_ge(w1_lo_ok, 2 * b)
                products(ps_31[:], 1, w1_hi, w1_lo, range(C // 2, C)).then_inc(mm[1], 1)

            def layer2(b):
                first = isinstance(b, int) and b == 0
                pe.wait_ge(x_hi_ok[2], b + 1)
                pe.wait_ge(*((unit_hi, W2 + C) if first else (w2_hi_ok, 2 * b)))
                sweep(ps_20[:], x_hi[2], w2_hi, opens=True)
                pe.wait_ge(*((unit_lo, W2 + C) if first else (w2_lo_ok, 2 * b)))
                sweep(ps_20[:], x_hi[2], w2_lo)
                pe.wait_ge(x_lo_ok[2], b + 1)
                sweep(ps_20[:], x_lo[2], w2_hi, closes=True).then_inc(mm[2], 1)

            def layer3_signs(b):
                pe.wait_ge(sign_ok, b + 1)
                before(pe, diff_ok, b)
                pe.wait_ge(x_hi_ok[3], b + 1)
                sweep(ps_sign[:], x_hi[spare(3, b)], sign, opens=True)
                pe.wait_ge(x_lo_ok[3], b + 1)
                sweep(ps_sign[:], x_lo[spare(3, b)], sign, closes=True).then_inc(mm_sign, 1)

            def layer3(b, chunks=range(C)):
                last = products(ps_31[:], spare(3, b), w3_hi, w3_lo, chunks)
                if C - 1 in chunks:
                    last.then_inc(mm[3], 1)

            def first_layer3():
                pe.wait_ge(unit_hi, W3 + C)
                sweep(ps_31[:], x_hi[3], w3_hi, opens=True)
                sweep(ps_31[:], x_lo[3], w3_hi)
                pe.wait_ge(unit_lo, W3 + C)
                sweep(ps_31[:], x_hi[3], w3_lo, closes=True).then_inc(mm[3], 1)

            def step(t):
                layer3_signs(t - 3)
                if isinstance(t, int) and t == 3:
                    first_layer3()
                else:
                    layer3(t - 3)
                x_turn(1, t - 1)
                layer2(t - 2)
                pe.wait_ge(a_ld, 16 * (t + 1))
                x_turn(0, t)
                a_turn(t)
                layer1(t - 1, lambda: x_turn(3, t - 2))
                layer0(t)
                x_turn(2, t - 1)

            pe.wait_ge(ident_ok, 1)
            for k in range(WARM_UP):
                nc.tensor.transpose(ps_31[:, 0:P], ident[:], ident[:])
            x_turn(0, 0)
            units_turn(base_raw, BASE, lambda k: (base_diag_ok, k + 1))
            a_turn(0)
            pe.wait_ge(ones_ok, 1)
            first_layer0()
            units_turn(as_loaded(w1_raw), W1, lambda k: (w1_first_ld[k], 16))
            a_turn(1)
            x_turn(1, 0)
            layer0(1)
            units_turn(as_loaded(w2_raw), W2, lambda k: (w2_first_ld[k], 16), range(0, C // 2))
            x_turn(0, 2)
            units_turn(as_loaded(w2_raw), W2, lambda k: (w2_first_ld[k], 16), range(C // 2, C - 1))
            layer1(0)
            a_turn(2)
            units_turn(as_loaded(w2_raw), W2, lambda k: (w2_first_ld[k], 16), range(C - 1, C))
            layer0(2, lambda: x_turn(2, 0))
            x_turn(1, 1)
            layer2(0)
            units_turn(w3_raw, W3, lambda k: (w3_diag_ok, k + 1), range(0, 2))
            layer1(1, lambda: x_turn(3, 0))
            units_turn(w3_raw, W3, lambda k: (w3_diag_ok, k + 1), range(2, C))
            x_turn(2, 1)
            step(3)
            with pe.Fori(*LOOP) as t:
                step(t)
            layer3_signs(NB - 3)
            layer3(NB - 3)
            x_turn(1, NB - 1)
            layer2(NB - 2)
            layer1(NB - 1, lambda: x_turn(3, NB - 2))
            layer3_signs(NB - 2)
            x_turn(2, NB - 1)
            layer3(NB - 2, range(C // 2))
            layer2(NB - 1)
            layer3(NB - 2, range(C // 2, C - 1))
            x_turn(3, NB - 1)
            layer3(NB - 2, range(C - 1, C))
            layer3_signs(NB - 1)
            for h, (a, e) in enumerate(cols):
                if h == 1:
                    pe.wait_ge(y_ok, NB - 1)
                products(ps_last[h][:, a:e], spare(3, NB - 1), w3_hi[:, :, a:e], w3_lo[:, :, a:e]).then_inc(mm[3], 1)


_INS = ['x', 'itok_B_6_15', 'itok_B_3_7', 'itok_B_1_14', 'condB_coeff', 'mask_Bx4096x4096_ik1',
        'L0_cond_base_weight', 'L0_cond_base_bias', 'L0_cond_lora_A_w', 'L0_cond_lora_B_w',
        'L1_cond_weight', 'L2_cond_weight', 'L3_cond_W', 'L3_cond_b']


def kernel(**inputs):
    import numpy as _np
    import concourse.bacc as _bacc
    from concourse import mybir as _mybir
    from concourse.bass_utils import run_bass_kernel_spmd as _run

    nc = _bacc.Bacc("TRN2", target_bir_lowering=False, num_devices=1)
    arrays, args = {}, []
    for name in _INS:
        a = _np.ascontiguousarray(inputs[name])
        arrays[f"in_{name}_dram"] = a
        args.append(nc.dram_tensor(f"in_{name}_dram", a.shape, _mybir.dt.from_np(a.dtype), kind="ExternalInput").ap())
    shape = inputs['x'].shape
    args.append(nc.dram_tensor("out_0_dram", shape, _mybir.dt.from_np(_np.dtype('float32')), kind="ExternalOutput").ap())
    adapter_chain(nc, *args)
    r = _run(nc, [arrays], core_ids=[0])
    return r.results[0]["out_0_dram"]
```
